# Optimizing a Trainium2 kernel written in Bass

```python
import numpy as np
import jax
import jax.numpy as jnp

def _softmax(x, axis=-1):
    return jax.nn.softmax(x, axis=axis)

def _gelu(x):
    return jax.nn.gelu(x, approximate=True)

def _silu(x):
    return jax.nn.silu(x)

def _sigmoid(x):
    return jax.nn.sigmoid(x)

def _layernorm(x, axis=-1, eps=1e-05):
    m = jnp.mean(x, axis=axis, keepdims=True)
    v = jnp.var(x, axis=axis, keepdims=True)
    return (x - m) / jnp.sqrt(v + eps)

def _scatter_add(tgt, idx, src, axis=0):
    return tgt.at[idx].add(src)

def _segment_sum(src, seg, n):
    return jax.ops.segment_sum(src, seg, n)
kernel_name = 'mk_xattn_ffn_d1_seqx_r4_ab06d1'

def setup_inputs(seed: int=0):
    np.random.seed(seed)
    _w = jnp.asarray

    def _rec_inputs():
        import jax
        import jax.numpy as jnp
        _rk = jax.random.key(seed)
        x = -0.0002928 + 1 * jax.random.normal(jax.random.fold_in(_rk, 1), (4, 1024, 256), jnp.float32)
        _lenS = 1024 - jax.random.randint(jax.random.fold_in(_rk, 7), (4,), 0, max(1, 1024 // 4) + 1, jnp.int32)
        _lenS2 = 64 - jax.random.randint(jax.random.fold_in(_rk, 8), (4,), 0, max(1, 64 // 4) + 1, jnp.int32)
        _ctx_1024P = jax.random.normal(jax.random.fold_in(_rk, 11), (4, 16, 256), jnp.float32)
        _ctx_1024c = jax.random.dirichlet(jax.random.fold_in(_rk, 511), 0.3 * jnp.ones((16,), jnp.float32), (4, 64))
        _ctx_1024t = jnp.einsum('bsk,bkd->bsd', _ctx_1024c, _ctx_1024P)
        _ctx_1024t = _ctx_1024t * jax.lax.rsqrt(jnp.mean(jnp.square(_ctx_1024t)) + 1e-12) * 0.953939
        ctx_1024 = -1.39393e-06 + 0.999914 * (_ctx_1024t + 0.3 * jax.random.normal(jax.random.fold_in(_rk, 611), (4, 64, 256), jnp.float32))
        _validS = jnp.arange(1024)[None, :] < _lenS[:, None]
        _validS2 = jnp.arange(64)[None, :] < _lenS2[:, None]
        _causal = jnp.tril(jnp.ones((1024, 1024), dtype=bool))
        mask_Bx1xSxS2_ik1 = jnp.where(jnp.broadcast_to(_validS2[:, None, None, :], (4, 1, 1024, 64)), 1, 0).astype(jnp.int32)
        return (x, ctx_1024, mask_Bx1xSxS2_ik1)
    x, ctx_1024, mask_Bx1xSxS2_ik1 = _rec_inputs()

    def _L0_xattn_setup():
        import jax, jax.numpy as jnp
        import numpy as np
        D_MODEL = 256
        H = 16
        D_K = D_MODEL // H
        B, S = (2, 512)
        key = jax.random.key(seed)
        ks = jax.random.split(key, 12)
        sd = 1.0 / np.sqrt(D_MODEL)
        return {'query': jax.random.normal(ks[0], (B, S, D_MODEL), dtype=jnp.float32), 'key': jax.random.normal(ks[1], (B, S, D_MODEL), dtype=jnp.float32), 'value': jax.random.normal(ks[2], (B, S, D_MODEL), dtype=jnp.float32), 'mask': jax.random.randint(ks[3], (B, 1, S, S), 0, 2, dtype=jnp.int32), 'Wq': jax.random.normal(ks[4], (D_MODEL, D_MODEL), dtype=jnp.float32) * sd, 'bq': jnp.zeros((D_MODEL,), dtype=jnp.float32), 'Wk': jax.random.normal(ks[5], (D_MODEL, D_K), dtype=jnp.float32) * sd, 'bk': jnp.zeros((D_K,), dtype=jnp.float32), 'Wv': jax.random.normal(ks[6], (D_MODEL, D_K), dtype=jnp.float32) * sd, 'bv': jnp.zeros((D_K,), dtype=jnp.float32), 'Wo': jax.random.normal(ks[7], (D_MODEL, D_MODEL), dtype=jnp.float32) * sd, 'bo': jnp.zeros((D_MODEL,), dtype=jnp.float32)}
    _L0_xattn_all = _L0_xattn_setup()
    _L0_xattn_in = {k: v for k, v in _L0_xattn_all.items() if k in ('Wq', 'bq', 'Wk', 'bk', 'Wv', 'bv', 'Wo', 'bo')}
    del _L0_xattn_all

    def _L0_ffn_setup():
        import jax, jax.numpy as jnp
        import numpy as np
        B, S, D = (4, 512, 256)
        P = 9
        DM = D // 4
        EPS = 1e-05

        def _mix(x, mix_kernel):
            xp = jnp.pad(x, ((0, 0), (1, 1), (0, 0)))
            return mix_kernel[0] * xp[:, :-2] + mix_kernel[1] * xp[:, 1:-1] + mix_kernel[2] * xp[:, 2:]

        def _layernorm(h, gamma, beta):
            mu = jnp.mean(h, axis=-1, keepdims=True)
            var = jnp.var(h, axis=-1, keepdims=True)
            return (h - mu) * jax.lax.rsqrt(var + EPS) * gamma + beta
        key = jax.random.key(seed)
        ks = jax.random.split(key, 12)
        sc_in = 1.0 / np.sqrt(D)
        sc_mid = 1.0 / np.sqrt(DM)
        return {'x': jax.random.normal(ks[0], (B, S, D), dtype=jnp.float32), 'mix_kernel': jax.random.normal(ks[1], (3, D), dtype=jnp.float32) * 0.5, 'W1': jax.random.normal(ks[2], (P, D, DM), dtype=jnp.float32) * sc_in, 'b1': jnp.zeros((P, DM), dtype=jnp.float32), 'W2': jax.random.normal(ks[3], (P, DM, D), dtype=jnp.float32) * sc_mid, 'b2': jnp.zeros((P, D), dtype=jnp.float32), 'Wo1': jax.random.normal(ks[4], (D, DM), dtype=jnp.float32) * sc_in, 'bo1': jnp.zeros((DM,), dtype=jnp.float32), 'Wo2': jax.random.normal(ks[5], (DM, P), dtype=jnp.float32) * sc_mid, 'bo2': jnp.zeros((P,), dtype=jnp.float32), 'gamma': jnp.ones((D,), dtype=jnp.float32), 'beta': jnp.zeros((D,), dtype=jnp.float32)}
    _L0_ffn_all = _L0_ffn_setup()
    _L0_ffn_in = {k: v for k, v in _L0_ffn_all.items() if k in ('mix_kernel', 'W1', 'b1', 'W2', 'b2', 'Wo1', 'bo1', 'Wo2', 'bo2', 'gamma', 'beta')}
    del _L0_ffn_all
    return {'x': x, 'ctx_1024': ctx_1024, 'mask_Bx1xSxS2_ik1': mask_Bx1xSxS2_ik1, 'L0_xattn_Wq': _L0_xattn_in['Wq'], 'L0_xattn_bq': _L0_xattn_in['bq'], 'L0_xattn_Wk': _L0_xattn_in['Wk'], 'L0_xattn_bk': _L0_xattn_in['bk'], 'L0_xattn_Wv': _L0_xattn_in['Wv'], 'L0_xattn_bv': _L0_xattn_in['bv'], 'L0_xattn_Wo': _L0_xattn_in['Wo'], 'L0_xattn_bo': _L0_xattn_in['bo'], 'L0_ffn_mix_kernel': _L0_ffn_in['mix_kernel'], 'L0_ffn_W1': _L0_ffn_in['W1'], 'L0_ffn_b1': _L0_ffn_in['b1'], 'L0_ffn_W2': _L0_ffn_in['W2'], 'L0_ffn_b2': _L0_ffn_in['b2'], 'L0_ffn_Wo1': _L0_ffn_in['Wo1'], 'L0_ffn_bo1': _L0_ffn_in['bo1'], 'L0_ffn_Wo2': _L0_ffn_in['Wo2'], 'L0_ffn_bo2': _L0_ffn_in['bo2'], 'L0_ffn_gamma': _L0_ffn_in['gamma'], 'L0_ffn_beta': _L0_ffn_in['beta']}

def reference(x, ctx_1024, mask_Bx1xSxS2_ik1, L0_xattn_Wq, L0_xattn_bq, L0_xattn_Wk, L0_xattn_bk, L0_xattn_Wv, L0_xattn_bv, L0_xattn_Wo, L0_xattn_bo, L0_ffn_mix_kernel, L0_ffn_W1, L0_ffn_b1, L0_ffn_W2, L0_ffn_b2, L0_ffn_Wo1, L0_ffn_bo1, L0_ffn_Wo2, L0_ffn_bo2, L0_ffn_gamma, L0_ffn_beta):
    import jax
    import jax.numpy as jnp

    def _L0_xattn_ref(query, key, value, mask, Wq, bq, Wk, bk, Wv, bv, Wo, bo):
        import jax, jax.numpy as jnp
        import numpy as np
        D_MODEL = 256
        H = 16
        D_K = D_MODEL // H
        B, S = (2, 512)
        b, s, _ = query.shape
        q = query @ Wq + bq
        k = key @ Wk + bk
        v = value @ Wv + bv
        q = q.reshape(b, s, H, D_K).transpose(0, 2, 1, 3)
        scores = jnp.einsum('bhqd,bkd->bhqk', q, k) / jnp.sqrt(jnp.float32(D_K))
        scores = jnp.where(mask == 0, jnp.float32(-1000000000.0), scores)
        attn = jax.nn.softmax(scores, axis=-1)
        x = jnp.einsum('bhqk,bkd->bhqd', attn, v)
        x = x.transpose(0, 2, 1, 3).reshape(b, s, H * D_K)
        return x @ Wo + bo

    def _L0_ffn_ref(x, mix_kernel, W1, b1, W2, b2, Wo1, bo1, Wo2, bo2, gamma, beta):
        import jax, jax.numpy as jnp
        import numpy as np
        B, S, D = (4, 512, 256)
        P = 9
        DM = D // 4
        EPS = 1e-05

        def _mix(x, mix_kernel):
            xp = jnp.pad(x, ((0, 0), (1, 1), (0, 0)))
            return mix_kernel[0] * xp[:, :-2] + mix_kernel[1] * xp[:, 1:-1] + mix_kernel[2] * xp[:, 2:]

        def _layernorm(h, gamma, beta):
            mu = jnp.mean(h, axis=-1, keepdims=True)
            var = jnp.var(h, axis=-1, keepdims=True)
            return (h - mu) * jax.lax.rsqrt(var + EPS) * gamma + beta
        x_mixed = _mix(x, mix_kernel)
        h = jnp.einsum('bsd,pdm->bspm', x_mixed, W1) + b1
        stacked_paths = jnp.einsum('bspm,pmd->bspd', h, W2) + b2
        scores = jnp.tanh(x_mixed @ Wo1 + bo1) @ Wo2 + bo2
        idx = jnp.argmax(scores, axis=-1)
        weights = jax.nn.one_hot(idx, P, dtype=stacked_paths.dtype)
        collapsed = jnp.einsum('bspd,bsp->bsd', stacked_paths, weights)
        return _layernorm(x + collapsed, gamma, beta)
    x = x + _L0_xattn_ref(_layernorm(x, axis=-1), ctx_1024, ctx_1024, mask_Bx1xSxS2_ik1, L0_xattn_Wq, L0_xattn_bq, L0_xattn_Wk, L0_xattn_bk, L0_xattn_Wv, L0_xattn_bv, L0_xattn_Wo, L0_xattn_bo)
    x = x + _L0_ffn_ref(_layernorm(x, axis=-1), L0_ffn_mix_kernel, L0_ffn_W1, L0_ffn_b1, L0_ffn_W2, L0_ffn_b2, L0_ffn_Wo1, L0_ffn_bo1, L0_ffn_Wo2, L0_ffn_bo2, L0_ffn_gamma, L0_ffn_beta)
    return x

_drawn_inputs = setup_inputs


def setup_inputs(seed=0):
    import zlib

    import numpy as np

    out = dict(_drawn_inputs(seed))
    spreads = {'L0_xattn_bq': (0.0, 0.1),
     'L0_xattn_bk': (0.0, 0.1),
     'L0_xattn_bv': (0.0, 0.1),
     'L0_xattn_bo': (0.0, 0.1),
     'L0_ffn_b1': (0.0, 0.1),
     'L0_ffn_b2': (0.0, 0.1),
     'L0_ffn_bo1': (0.0, 0.1),
     'L0_ffn_bo2': (0.0, 0.1),
     'L0_ffn_gamma': (1.0, 0.2),
     'L0_ffn_beta': (0.0, 0.1)}
    factors = {}
    for name, (base, spread) in spreads.items():
        noise = np.random.default_rng([zlib.crc32(name.encode()), seed]).standard_normal(out[name].shape)
        drawn = base * np.exp(spread * noise) if base else spread * noise
        out[name] = jnp.asarray(drawn.astype(out[name].dtype))
    for name, factor in factors.items():
        out[name] = (out[name] * factor).astype(out[name].dtype)
    return out
```

```python
from contextlib import ExitStack

import numpy as np

import concourse.bass as bass
from concourse import mybir

F32 = mybir.dt.float32
F32R = mybir.dt.float32r
BF16 = mybir.dt.bfloat16
I32 = mybir.dt.int32
ALU = mybir.AluOpType
ACT = mybir.ActivationFunctionType
AX = mybir.AxisListType

P = 128
B, S, D = 4, 1024, 256
SK = 64
H, DK = 16, 16
NPATH, DM = 9, 64
CH = 512
NJ = S // CH
NT = CH // P
KD = D // P
NQ = 4
NPAIR = H // 2
NM = 5
EPS = 1e-5
MASKED = -float(2.0 ** 100)

C_ID = 0
C_D4 = C_ID + P
C_IDK = C_D4 + 4 * SK
C_SEL = C_IDK + 4 * SK
C_E = C_SEL + NQ * 4 * SK
C_BC = C_E + NPAIR * 32
C_VM = C_BC + KD * NT * P
C_IO = C_VM + 32
C_N = C_IO + NPATH


def constants():
    c = np.zeros((P, C_N), np.float32)
    r = np.arange(P)[:, None]
    hk = np.arange(4 * SK)[None, :]
    c[:, C_ID:C_ID + P] = np.eye(P)
    c[:, C_D4:C_D4 + 4 * SK] = (r % 64) // DK == hk // SK
    c[:, C_IDK:C_IDK + 4 * SK] = r % 64 == hk % SK
    for q in range(NQ):
        c[:, C_SEL + q * 4 * SK:C_SEL + (q + 1) * 4 * SK] = (r % 64 < 32) & (r % 16 == 4 * q + hk // SK)
    for p in range(NPAIR):
        c[:, C_E + 32 * p:C_E + 32 * p + 32] = np.arange(32)[None, :] % 16 == 2 * p + r // 64
    for m in range(KD):
        for k in range(NT):
            at = C_BC + P * (m * NT + k)
            c[:, at:at + P] = r == 32 * k + 8 * m + np.arange(P)[None, :] // DK
    c[:, C_VM:C_VM + 32] = r // 64 == np.arange(32)[None, :] // DK
    c[:, C_IO:C_IO + NPATH] = np.arange(NPATH) - NPATH
    return c


def layer_program(nc, x, ctx, mask, Wq, bq, Wk, bk, Wv, bv, Wo, bo, mixk, W1, b1, W2, b2,
                  Wo1, bo1, Wo2, bo2, gamma, beta, consts, out):
    with ExitStack() as stack:
        def sb(name, shape, dt=F32):
            return stack.enter_context(nc.sbuf_tensor(name, shape, dt))

        def sem(name):
            return stack.enter_context(nc.semaphore(name))

        stack.enter_context(nc.allow_non_contiguous_dma("biases, one value per partition"))

        cst = sb("cst", [P, C_N])
        ident_b = sb("ident_b", [P, P], BF16)
        wqh, wql = sb("wqh", [P, KD, D], F32R), sb("wql", [P, KD, D], F32R)
        w1h, w1l = sb("w1h", [P, KD, NM * P], F32R), sb("w1l", [P, KD, NM * P], F32R)
        w2 = sb("w2", [P, NM, D])
        wo = sb("wo", [P, KD, D])
        wo2 = sb("wo2", [P, NPATH])
        wk = sb("wk", [P, KD, DK])
        wk8 = sb("wk8", [P, KD, P])
        wv = sb("wv", [P, KD, DK])
        bqs = sb("bqs", [P, KD])
        bks = sb("bks", [P, 1])
        bvs = sb("bvs", [P, DK])
        bos, gms, bts = sb("bos", [P, D]), sb("gms", [P, D]), sb("bts", [P, D])
        b1s = sb("b1s", [P, NM])
        bo2s = sb("bo2s", [P, NPATH])
        mks = sb("mks", [P, 3, KD])
        unused = sb("unused", [P, 3])
        halfneg = sb("halfneg", [P, NT])
        ctx_in = sb("ctx_in", [SK, B, D])
        ctxT = sb("ctxT", [P, KD, B, 2, SK])
        khi = sb("khi", [P, B, SK], F32R)
        klo = sb("klo", [P, B, SK])
        krep = sb("krep", [P, B, SK])
        vall = sb("vall", [P, B, DK])
        kmh = sb("kmh", [P, 2, 4 * SK], F32R)
        kml = sb("kml", [P, 2, 4 * SK], F32R)
        kms = sb("kms", [P, NQ, 4 * SK], F32R)
        vd = sb("vd", [P, 2 * DK])
        def ln_buffers(n):
            return (sb(f"st{n}", [P, NT, 2, 3]), sb(f"su{n}", [P, NT, 3]), sb(f"dm{n}", [P, NT]), sb(f"mu{n}", [P, NT]),
                    sb(f"va{n}", [P, NT]), sb(f"vb{n}", [P, NT]), sb(f"ve{n}", [P, NT]), sb(f"rs{n}", [P, NT]))

        xin = sb("xin", [P, NJ, NT, D])
        min_ = sb("min_", [P, NJ, NT, SK], I32)
        xb = sb("xb", [P, NJ, NT, D])
        mb = sb("mb", [P, NT, 2, SK])
        mT = sb("mT", [P, CH], F32R)
        ln1 = ln_buffers("1")
        ln2 = ln_buffers("2")
        ln3 = ln_buffers("3")
        xh1 = sb("xh1", [P, NT, D])
        xTh, xTl = sb("xTh", [P, KD, CH], F32R), sb("xTl", [P, KD, CH], F32R)
        qh = sb("qh", [P, NQ, CH], F32R)
        ql = sb("ql", [P, NQ, CH], F32R)
        mx = sb("mx", [P, NT, H])
        nm = sb("nm", [P, NT, 2 * H], F32R)
        nmT = sb("nmT", [32, CH], F32R)
        e = sb("e", [P, NPAIR, CH])
        rD = sb("rD", [P, P])
        osb = sb("osb", [P, KD, CH])
        oT = sb("oT", [P, KD, CH])
        x1 = sb("x1", [P, NJ, NT, D])
        xh2 = sb("xh2", [P, NJ, NT, D])
        x2T = sb("x2T", [P, KD, S + 2])
        xm = sb("xm", [P, KD, CH])
        xmh, xml = sb("xmh", [P, KD, S], F32R), sb("xml", [P, KD, S], F32R)
        hs = sb("hs", [P, NM, CH])
        h4s = sb("h4s", [P, CH])
        wq32 = h4s[:, :].rearrange("p (c n) -> p c n", c=KD)
        w1_32 = hs[:, :, :].rearrange("p m t -> p (m t)")[:, 0:KD * NM * P].rearrange("p (c n) -> p c n", c=KD)
        thT = sb("thT", [P, CH])
        gs = sb("gs", [P, NT, NPATH])
        gmax = sb("gmax", [P, NT])
        cand = sb("cand", [P, NT, NPATH])
        gidx = sb("gidx", [P, NT])
        oh = sb("oh", [P, NT, NPATH + 1], BF16)
        x1b = sb("x1b", [P, NT, D])
        res = sb("res", [P, NT, D])
        y = sb("y", [P, NT, D])

        ps = stack.enter_context(nc.psum_tensor("ps", [P, 8, CH], F32))

        ident = cst[:, C_ID:C_ID + P]

        s_cst, s_wa, s_wf = sem("consts_loaded"), sem("attn_weights_loaded"), sem("ffn_weights_loaded")
        s_x = [sem(f"x_loaded{j}") for j in range(NJ)]
        s_m = [sem(f"mask_loaded{j}") for j in range(NJ)]
        s_init = sem("memsets_done")
        s_wqh, s_wql, s_w1h, s_w1l = sem("wq_hi"), sem("wq_lo"), sem("w1_hi"), sem("w1_lo")
        s_id = sem("identity_in_bf16")
        s_setup_pe, s_setup_v = sem("setup_products"), sem("setup_copies")
        s_km = sem("score_operands_built")
        s_ln1s, s_ln1h, s_ln1p = sem("ln1_stats"), sem("ln1_halves"), sem("ln1_var_parts")
        s_ln1v, s_ln1r, s_ln1 = sem("ln1_var"), sem("ln1_rstd"), sem("ln1_done")
        s_ln2s, s_ln2h, s_ln2p = sem("ln2_stats"), sem("ln2_halves"), sem("ln2_var_parts")
        s_ln2v, s_ln2r, s_ln2 = sem("ln2_var"), sem("ln2_rstd"), sem("ln2_done")
        s_ln3s, s_ln3h, s_ln3p = sem("ln3_stats"), sem("ln3_halves"), sem("ln3_var_parts")
        s_ln3v, s_ln3r, s_ln3 = sem("ln3_var"), sem("ln3_rstd"), sem("ln3_done")
        s_mb, s_xb = sem("mask_bias"), sem("x_plus_bo")
        s_mTp, s_mT = sem("maskT_in_psum"), sem("maskT_copied")
        s_mrow = sem("mask_rows_placed")
        s_xTp, s_xTh, s_xTl = sem("xT_in_psum"), sem("xT_hi"), sem("xT_lo")
        s_qp, s_qh, s_ql = sem("q_in_psum"), sem("q_hi"), sem("q_lo")
        s_sn, s_mx = sem("scores_for_max"), sem("max_taken")
        s_nmh, s_nm = sem("negmax_hi"), sem("negmax_split")
        s_nTp, s_nT, s_nrow = sem("negmaxT_in_psum"), sem("negmaxT_copied"), sem("negmax_rows_placed")
        s_st, s_e = sem("scoresT_in_psum"), sem("exp_done")
        s_o, s_dn, s_osb = sem("pv_in_psum"), sem("denominators_in_psum"), sem("pv_copied")
        s_rd, s_bc, s_oT = sem("denominators_inverted"), sem("inverse_spread"), sem("attn_normalised")
        s_wo, s_x1 = sem("wo_in_psum"), sem("x1_done")
        s_x2p, s_x2T = sem("x2T_in_psum"), sem("x2T_copied")
        s_mix1, s_mix2, s_xm = sem("mix_one_term"), sem("mix_two_terms"), sem("mixed")
        s_xmh, s_xml = sem("mixed_hi"), sem("mixed_lo")
        s_f, s_fa, s_fv = sem("ffn_slot_filled"), sem("ffn_slot_read_by_act"), sem("ffn_slot_read_by_dve")
        s_g1, s_g2, s_g3, s_g4, s_oh = sem("gate_scores"), sem("gate_max"), sem("gate_cand"), sem("gate_index"), sem("onehot")
        s_res, s_x1b, s_yg, s_yo = sem("ffn_residual"), sem("x1_plus_beta"), sem("times_gamma"), sem("out_ready")
        s_w2 = sem("w2_reads_done")
        s_out = [sem(f"out_stored{j}") for j in range(NJ)]

        def at(b, per_row, n):
            return b * per_row + n

        xr = x.rearrange("b (j k p) d -> p b j k d", p=P, k=NT)
        outr = out.rearrange("b (j k p) d -> p b j k d", p=P, k=NT)
        mr = mask.rearrange("b o (j k p) s -> p (b o) j k s", p=P, k=NT)

        def halves(par):
            return (slice(0, 64), slice(64, 128)) if par == 0 else (slice(64, 128), slice(0, 64))

        def row_broadcast(vec, n, parts=P):
            return vec.rearrange("(o n) -> o n", o=1).broadcast_to([parts, n])

        USES = ["h4", "h0", "h1", "gate", "h2", "h3", "rep0", "rep1", "rep2", "rep3", "rep4", "w2a", "w2b"]
        NU = len(USES)
        BY_ACT = [u in ("h4", "h0", "h1", "h2", "h3") for u in USES]
        NFA, NFV = sum(BY_ACT), NU - sum(BY_ACT)

        def slot(j, u):
            n = j * NU + USES.index(u)
            return n, 6 + n % 2

        def reads_before(n, by_act):
            return sum(BY_ACT[i % NU] == by_act for i in range(n))

        block = stack.enter_context(nc.Block())

        @block.sync
        def _(sp):
            def load(dst, src, s):
                sp.dma_start(dst, src).then_inc(s, 16)

            load(cst[:, :], consts, s_cst)
            load(xin[:, 0], xr[:, 0, 0], s_x[0])
            load(min_[:, 0], mr[:, 0, 0], s_m[0])
            load(ctx_in[:, :, :], ctx.rearrange("b s d -> s b d"), s_wa)
            load(wk[:, :, :], Wk.rearrange("(c p) n -> p c n", p=P), s_wa)
            load(wv[:, :, :], Wv.rearrange("(c p) n -> p c n", p=P), s_wa)
            load(wq32, Wq.rearrange("(c p) n -> p c n", p=P), s_wa)
            load(bqs[:, :], bq.rearrange("(c p) -> p c", p=P), s_wa)
            for h in range(P // DK):
                load(bks[h * DK:(h + 1) * DK, :], bk.rearrange("(p o) -> p o", o=1), s_wa)
            load(bvs[:, :], row_broadcast(bv, DK), s_wa)
            load(bos[:, :], row_broadcast(bo, D), s_wa)
            load(wo[:, :, :], Wo.rearrange("(c p) n -> p c n", p=P), s_wa)
            load(xin[:, 1], xr[:, 0, 1], s_x[1])
            load(min_[:, 1], mr[:, 0, 1], s_m[1])
            for p in range(NPATH):
                load(w1_32[:, :, p * DM:(p + 1) * DM], W1[p].rearrange("(c p) m -> p c m", p=P), s_wf)
            load(w1_32[:, :, NPATH * DM:], Wo1.rearrange("(c p) m -> p c m", p=P), s_wf)
            load(w2[:, 0:4, :], W2[0:8].rearrange("(t a) m d -> (a m) t d", a=2), s_wf)
            load(w2[0:DM, 4, :], W2[8], s_wf)
            load(w2[DM:DM + NPATH, 4, :], b2, s_wf)
            load(wo2[DM:, :], Wo2, s_wf)
            load(b1s[:, 0:4], b1[0:8].rearrange("(t a) m -> (a m) t", a=2), s_wf)
            load(b1s[0:DM, 4:5], b1[8].rearrange("(m o) -> m o", o=1), s_wf)
            load(b1s[DM:, 4:5], bo1.rearrange("(m o) -> m o", o=1), s_wf)
            load(bo2s[:, :], row_broadcast(bo2, NPATH), s_wf)
            load(mks[:, :, :], mixk.rearrange("t (c p) -> p t c", p=P), s_wf)
            load(gms[:, :], row_broadcast(gamma, D), s_wf)
            load(bts[:, :], row_broadcast(beta, D), s_wf)

            def place_rows(b, j):
                sp.wait_ge(s_st, at(b, NJ * NPAIR, j * NPAIR))
                sp.wait_ge(s_mT, at(b, NJ, j + 1))
                for par in range(2):
                    _, mrow = halves(par)
                    for q in (par, par + 2):
                        sp.dma_start(qh[mrow, q, :].bitcast(F32), mT[mrow, :].bitcast(F32)).then_inc(s_mrow, 16)
                sp.wait_ge(s_nT, at(b, NJ, j + 1))
                for par in range(2):
                    r0 = halves(par)[1].start
                    for q in (par, par + 2):
                        sp.dma_start(ql[r0:r0 + 32, q, :].bitcast(F32), nmT[:, :].bitcast(F32)).then_inc(s_nrow, 16)

            def next_inputs(b, j):
                sp.wait_ge(s_ln1, at(b, NJ, j + 1))
                sp.wait_ge(s_xb, at(b, NJ, j + 1))
                sp.dma_start(xin[:, j], xr[:, b + 1, j]).then_inc(s_x[j], 16)
                sp.wait_ge(s_mb, at(b, NJ, j + 1))
                sp.dma_start(min_[:, j], mr[:, b + 1, j]).then_inc(s_m[j], 16)

            def store(b, j):
                sp.wait_ge(s_yo, 1 + at(b, NJ, j + 1))
                sp.dma_start(outr[:, b, j], y[:, :, :]).then_inc(s_out[j], 16)

            for j in range(NJ):
                next_inputs(0, j)
                place_rows(0, j)
            with sp.Fori(1, B - 1) as b:
                for j in range(NJ):
                    next_inputs(b, j)
                    place_rows(b, j)
                    store(b - 1, j)
            for j in range(NJ):
                place_rows(B - 1, j)
                store(B - 2, j)
            for j in range(NJ):
                store(B - 1, j)
            for j in range(NJ):
                sp.wait_ge(s_out[j], 16 * B + (16 if j == NJ - 1 else 0))

        @block.tensor
        def _(pe):
            def three_pass(out_, lhs, rhs, more):
                terms = [(lhs[0], rhs[0]), (lhs[0], rhs[1]), (lhs[1], rhs[0])]
                n = 0
                for a, c in terms:
                    for k in range(KD):
                        n += 1
                        mm = nc.tensor.matmul(out_, a(k), c(k), start=(n == 1),
                                              stop=(n == 3 * KD and not more))
                return mm

            pe.wait_ge(s_cst, 16)
            pe.wait_ge(s_wa, 16 * WA_LOADS)
            for b in range(B):
                for k in range(KD):
                    i = (k * B + b) * SK
                    mm = nc.tensor.transpose(ps[:, 0, i:i + SK], ctx_in[:, b, k * P:(k + 1) * P], ident[0:SK, 0:SK])
            mm.then_inc(s_setup_pe, 1)
            pe.wait_ge(s_setup_v, 2)
            for k in range(KD):
                mm = nc.tensor.matmul(ps[:, 1, 0:B * SK].rearrange("p (b s) -> p b s", b=B), wk8[:, k, :],
                                      ctxT[:, k, :, 0, :], start=(k == 0), stop=(k == KD - 1))
            mm.then_inc(s_setup_pe, 1)
            for b in range(B):
                for k in range(KD):
                    mm = nc.tensor.matmul(ps[:, 2, b * DK:(b + 1) * DK], ctxT[:, k, b, :, :], wv[:, k, :],
                                          start=(k == 0), stop=(k == KD - 1))
            mm.then_inc(s_setup_pe, 1)

            def t1(b, j):
                pe.wait_ge(s_mb, at(b, NJ, j + 1))
                pe.wait_ge(s_rd, at(b, NJ, j))
                for k in range(NT):
                    mm = nc.tensor.transpose(ps[:, 2, k * P:(k + 1) * P], mb[:, k, :, :], ident)
                mm.then_inc(s_mTp, 1)
                pe.wait_ge(s_ln1, at(b, NJ, j + 1))
                pe.wait_ge(s_x2T, at(b, NJ, j))
                for c in range(KD):
                    for k in range(NT):
                        mm = nc.tensor.transpose(ps[:, c, k * P:(k + 1) * P], xh1[:, k, c * P:(c + 1) * P], ident)
                mm.then_inc(s_xTp, 1)

            def wq(b, j):
                pe.wait_ge(s_xTl, at(b, NJ, j + 1))
                for m in range(KD):
                    ms = slice(m * P, (m + 1) * P)
                    mm = three_pass(ps[:, m, :], (lambda k: wqh[:, k, ms], lambda k: wql[:, k, ms]),
                                    (lambda k: xTh[:, k, :], lambda k: xTl[:, k, :]), False)
                    mm.then_inc(s_qp, 1)

            def scores_for_max(b, j):
                pe.wait_ge(s_qh, at(b, NJ, j + 1))
                pe.wait_ge(s_mrow, at(b, 16 * NJ * NQ, (j + 1) * NQ * 16))
                pe.wait_ge(s_km, at(b, 3, 3))
                pe.wait_ge(s_oT, at(b, NJ, j))
                pe.wait_ge(s_mT, at(b, NJ, j + 1))
                for k in range(NT):
                    if k >= 2:
                        pe.wait_ge(s_mx, at(b, NJ * NT, j * NT + k - 1))
                    for q in range(NQ):
                        bank = 2 + 2 * (k % 2) + q // 2
                        mm = nc.tensor.matmul(ps[:, bank, (q % 2) * 256:(q % 2 + 1) * 256],
                                              qh[:, q, k * P:(k + 1) * P], kmh[:, q % 2, :],
                                              start=True, stop=True)
                    mm.then_inc(s_sn, 1)

            def negmax_transposed(b, j):
                pe.wait_ge(s_nm, at(b, NJ, j + 1))
                pe.wait_ge(s_ql, at(b, NJ, j + 1))
                for k in range(NT):
                    mm = nc.tensor.transpose(ps[0:32, 0, k * P:(k + 1) * P], nm[:, k, :].bitcast(F32), ident)
                mm.then_inc(s_nTp, 1)

            def scores_transposed(b, j):
                pe.wait_ge(s_nrow, at(b, 16 * NJ * NQ, (j + 1) * NQ * 16))
                pe.wait_ge(s_mx, at(b, NJ * NT, (j + 1) * NT))
                for p in range(NPAIR):
                    q, c = p // 2, slice((p % 2) * P, (p % 2 + 1) * P)
                    bank = 2 + p % 4
                    if p >= 4 and p % 2 == 0:
                        pe.wait_ge(s_e, at(b, NJ * 4, j * 4 + p // 2 - 1))
                    nc.tensor.matmul(ps[:, bank, :], kmh[:, q % 2, c], qh[:, q, :], start=True, stop=False)
                    nc.tensor.matmul(ps[:, bank, :], kml[:, q % 2, c], qh[:, q, :], start=False, stop=False)
                    nc.tensor.matmul(ps[:, bank, :], kms[:, q, c], ql[:, q, :],
                                     start=False, stop=True).then_inc(s_st, 1)

            def pv(b, j):
                pe.wait_ge(s_nT, at(b, NJ, j + 1))
                for half in range(2):
                    pe.wait_ge(s_e, at(b, NJ * 4, j * 4 + 2 * half + 2))
                    for p in range(4):
                        mm = nc.tensor.matmul(ps[32 * p:32 * p + 32, half, :], vd[:, :], e[:, 4 * half + p, :],
                                              start=True, stop=True)
                mm.then_inc(s_o, 1)
                for p in range(NPAIR):
                    for k in range(NT):
                        mm = nc.tensor.matmul(ps[32 * k:32 * k + 32, 2, 0:P], cst[:, C_E + 32 * p:C_E + 32 * p + 32],
                                              e[:, p, k * P:(k + 1) * P], start=(p == 0), stop=(p == NPAIR - 1))
                mm.then_inc(s_dn, 1)

            def spread(b, j):
                pe.wait_ge(s_rd, at(b, NJ, j + 1))
                for c in range(KD):
                    for k in range(NT):
                        w = C_BC + (c * NT + k) * P
                        mm = nc.tensor.matmul(ps[:, 4 + c, k * P:(k + 1) * P], cst[:, w:w + P], rD[:, :],
                                              start=True, stop=True)
                mm.then_inc(s_bc, 1)

            def project_out(b, j):
                pe.wait_ge(s_osb, at(b, NJ, j + 1))
                pe.wait_ge(s_oT, at(b, NJ, j + 1))
                for k in range(NT):
                    for c in range(KD):
                        mm = nc.tensor.matmul(ps[:, k // 2, (k % 2) * D:(k % 2 + 1) * D], oT[:, c, k * P:(k + 1) * P],
                                              wo[:, c, :], start=(c == 0), stop=(c == KD - 1))
                mm.then_inc(s_wo, 1)

            def t2(b, j):
                pe.wait_ge(s_ln2, at(b, NJ, j + 1))
                for c in range(KD):
                    for k in range(NT):
                        mm = nc.tensor.transpose(ps[:, c, k * P:(k + 1) * P], xh2[:, j, k, c * P:(c + 1) * P], ident)
                mm.then_inc(s_x2p, 1)

            def take_slot(b, j, u):
                n, bank = slot(j, u)
                before = n - 2
                by_act = BY_ACT[before % NU]
                if by_act:
                    pe.wait_ge(s_fa, at(b, NJ * NFA, reads_before(before + 1, True)))
                elif before < 0:
                    pe.wait_ge(s_fv, 1 + at(b, NJ * NFV, 0))
                else:
                    pe.wait_ge(s_fv, 1 + at(b, NJ * NFV, reads_before(before + 1, False)))
                return ps[:, bank, :]

            def w1(b, j, m):
                o = take_slot(b, j, f"h{m}")
                js, ms = slice(j * CH, (j + 1) * CH), slice(m * P, (m + 1) * P)
                three_pass(o, (lambda k: w1h[:, k, ms], lambda k: w1l[:, k, ms]),
                           (lambda k: xmh[:, k, js], lambda k: xml[:, k, js]), False).then_inc(s_f, 1)

            def gate(b, j):
                o = take_slot(b, j, "gate")
                pe.wait_ge(s_fa, at(b, NJ * NFA, j * NFA + 1))
                for k in range(NT):
                    mm = nc.tensor.matmul(o[:, k * NPATH:(k + 1) * NPATH], thT[DM:, k * P:(k + 1) * P],
                                          wo2[DM:, :], start=True, stop=True)
                mm.then_inc(s_f, 1)

            def rep(b, j, m):
                o = take_slot(b, j, f"rep{m}")
                if m == 0:
                    pe.wait_ge(s_oh, at(b, NJ, j + 1))
                for k in range(NT):
                    ks = slice(k * P, (k + 1) * P)
                    for a in range(2):
                        p = 2 * m + a
                        if p < NPATH:
                            sel = oh[:, k, p:p + 1].broadcast_to([P, DM])
                            mm = nc.tensor.matmul(o[a * DM:(a + 1) * DM, ks], sel, ident_b[:, :], start=True, stop=True)
                        else:
                            mm = nc.tensor.matmul(o[DM:DM + NPATH, ks], oh[:, k, 0:NPATH], ident_b[:, :],
                                                  start=True, stop=True)
                mm.then_inc(s_f, 1)

            def w2_product(b, j):
                for i, u in enumerate(("w2a", "w2b")):
                    o = take_slot(b, j, u)
                    if i == 0:
                        pe.wait_ge(s_fv, 1 + at(b, NJ * NFV, j * NFV + 6))
                    for k in (2 * i, 2 * i + 1):
                        for m in range(NM):
                            n = P if m < 4 else DM + NPATH
                            h = hs[:, m, k * P:(k + 1) * P] if m < 4 else h4s[0:n, k * P:(k + 1) * P]
                            mm = nc.tensor.matmul(o[:, (k % 2) * D:(k % 2 + 1) * D], h,
                                                  w2[0:n, m, :], start=(m == 0), stop=(m == NM - 1))
                    mm.then_inc(s_f, 1)

            def step(ba, bf):
                for j in range(NJ):
                    if ba is not None:
                        t1(ba, j)
                    if bf is not None:
                        if j == 0:
                            pe.wait_ge(s_xmh, at(bf, NJ * KD, NJ * KD))
                            pe.wait_ge(s_xml, at(bf, NJ * KD, NJ * KD))
                        w1(bf, j, 4)
                        w1(bf, j, 0)
                        w1(bf, j, 1)
                    if ba is not None:
                        wq(ba, j)
                    if bf is not None:
                        gate(bf, j)
                        w1(bf, j, 2)
                        w1(bf, j, 3)
                    if ba is not None:
                        scores_for_max(ba, j)
                    if bf is not None:
                        for m in range(NM):
                            rep(bf, j, m)
                    if ba is not None:
                        negmax_transposed(ba, j)
                    if bf is not None:
                        w2_product(bf, j)
                    if ba is not None:
                        scores_transposed(ba, j)
                        pv(ba, j)
                        spread(ba, j)
                        project_out(ba, j)
                        t2(ba, j)

            pe.wait_ge(s_wqh, 1)
            pe.wait_ge(s_wql, 1)
            pe.wait_ge(s_setup_v, 5)
            step(0, None)
            pe.wait_ge(s_w1h, 1)
            pe.wait_ge(s_w1l, 1)
            pe.wait_ge(s_id, 1)
            with pe.Fori(1, B) as b:
                step(b, b - 1)
            step(None, B - 1)

        @block.scalar
        def _(act):
            act.wait_ge(s_wa, 16 * WA_LOADS)
            nc.scalar.activation(wqh[:, :, :], wq32, ACT.Copy).then_inc(s_wqh, 1)
            act.wait_ge(s_wf, 16 * WF_LOADS)
            nc.scalar.activation(w1h[:, :, :], w1_32, ACT.Copy).then_inc(s_w1h, 1)

            def copies_t1(b, j):
                act.wait_ge(s_mTp, at(b, NJ, j + 1))
                act.wait_ge(s_mrow, at(b, 16 * NJ * NQ, j * NQ * 16))
                nc.scalar.activation(mT[:, :], ps[:, 2, :], ACT.Copy).then_inc(s_mT, 1)
                act.wait_ge(s_xTp, at(b, NJ, j + 1))
                act.wait_ge(s_qp, at(b, NJ * KD, j * KD))
                for c in range(KD):
                    nc.scalar.activation(xTh[:, c, :], ps[:, c, :], ACT.Copy).then_inc(s_xTh, 1)

            def q_hi(b, j):
                act.wait_ge(s_st, at(b, NJ * NPAIR, j * NPAIR))
                for m in range(KD):
                    act.wait_ge(s_qp, at(b, NJ * KD, j * KD + m + 1))
                    for par in range(2):
                        r, _ = halves(par)
                        a = nc.scalar.activation(qh[r, 2 * m + par, :], ps[r, m, :], ACT.Identity, bias=bqs[r, m:m + 1])
                a.then_inc(s_qh, 1)

            def maxima(b, j):
                act.wait_ge(s_nTp, at(b, NJ, j + 1))
                act.wait_ge(s_nrow, at(b, 16 * NJ * NQ, j * NQ * 16))
                nc.scalar.activation(nmT[:, :], ps[0:32, 0, :], ACT.Copy).then_inc(s_nT, 1)

            def softmax_exp(b, j):
                act.wait_ge(s_dn, at(b, NJ, j))
                for i in range(4):
                    act.wait_ge(s_st, at(b, NJ * NPAIR, j * NPAIR + 2 * i + 2))
                    bank = 2 + 2 * (i % 2)
                    nc.scalar.activation(e[:, 2 * i:2 * i + 2, :], ps[:, bank:bank + 2, :], ACT.Exp).then_inc(s_e, 1)

            def pv_copy(b, j):
                act.wait_ge(s_o, at(b, NJ, j + 1))
                act.wait_ge(s_oT, at(b, NJ, j))
                nc.scalar.activation(osb[:, :, :], ps[:, 0:2, :], ACT.Copy).then_inc(s_osb, 1)

            def copy_t2(b, j):
                act.wait_ge(s_x2p, at(b, NJ, j + 1))
                act.wait_ge(s_xm, at(b, NJ * KD, 0))
                nc.scalar.activation(x2T[:, :, 1 + j * CH:1 + (j + 1) * CH], ps[:, 0:2, :], ACT.Copy).then_inc(s_x2T, 1)

            def mixed_hi(b, j):
                for c in range(KD):
                    act.wait_ge(s_xm, at(b, NJ * KD, j * KD + c + 1))
                    nc.scalar.activation(xmh[:, c, j * CH:(j + 1) * CH], xm[:, c, :], ACT.Copy).then_inc(s_xmh, 1)

            def hidden(b, j, m):
                n, bank = slot(j, f"h{m}")
                act.wait_ge(s_f, at(b, NJ * NU, n + 1))
                if m == 4:
                    act.wait_ge(s_fv, 1 + at(b, NJ * NFV, j * NFV))
                    nc.scalar.activation(thT[DM:, :], ps[DM:, bank, :], ACT.Tanh, bias=b1s[DM:, 4:5])
                    nc.scalar.activation(hs[0:DM, 4, :], ps[0:DM, bank, :], ACT.Identity,
                                         bias=b1s[0:DM, 4:5]).then_inc(s_fa, 1)
                else:
                    nc.scalar.activation(hs[:, m, :], ps[:, bank, :], ACT.Identity, bias=b1s[:, m:m + 1]).then_inc(s_fa, 1)

            def step(ba, bf):
                if bf is not None:
                    for j in range(NJ):
                        mixed_hi(bf, j)
                for j in range(NJ):
                    if ba is not None:
                        copies_t1(ba, j)
                    if bf is not None:
                        hidden(bf, j, 4)
                        hidden(bf, j, 0)
                        hidden(bf, j, 1)
                    if ba is not None:
                        q_hi(ba, j)
                    if bf is not None:
                        hidden(bf, j, 2)
                        hidden(bf, j, 3)
                    if ba is not None:
                        maxima(ba, j)
                        softmax_exp(ba, j)
                        pv_copy(ba, j)
                        copy_t2(ba, j)

            step(0, None)
            act.wait_ge(s_w1l, 1)
            with act.Fori(1, B) as b:
                step(b, b - 1)
            step(None, B - 1)

        @block.vector
        def _(dve):
            v = nc.vector
            dve.wait_ge(s_cst, 16)
            v.tensor_copy(ident_b[:, :], ident).then_inc(s_id, 1)
            v.memset(kml[:, :, :].bitcast(F32), 0.0).then_inc(s_fv, 1)
            v.memset(ql[:, :, :].bitcast(F32), 0.0)
            v.memset(x2T[:, :, 0:1], 0.0)
            v.memset(x2T[:, :, S + 1:S + 2], 0.0)
            v.memset(oh[:, :, :], 0.0)
            v.memset(hs[DM:, 4, :], 1.0)
            for q in range(NQ):
                _, m = halves(q % 2)
                v.tensor_copy(kms[m, q, :], cst[m, C_SEL + q * 256:C_SEL + (q + 1) * 256])
            for par in range(2):
                _, m = halves(par)
                a = v.tensor_copy(kmh[m, par, :], cst[m, C_IDK:C_IDK + 256])
            a.then_inc(s_init, 1)

            dve.wait_ge(s_wa, 16 * WA_LOADS)
            v.tensor_copy(wk8[:, :, :].rearrange("p c (h d) -> p c h d", h=8),
                          wk[:, :, :].rearrange("p c (h d) -> p c h d", h=1).broadcast_to([P, KD, 8, DK])).then_inc(s_setup_v, 1)
            dve.wait_ge(s_setup_pe, 1)
            for a in range(2):
                ins = v.tensor_copy(ctxT[:, :, :, a, :], ps[:, 0, :].rearrange("p (c b s) -> p c b s", c=KD, b=B))
            ins.then_inc(s_setup_v, 1)
            dve.wait_ge(s_setup_pe, 2)
            v.tensor_scalar(krep[:, :, :], ps[:, 1, 0:B * SK].rearrange("p (b s) -> p b s", b=B), bks[:, 0:1],
                            float(DK) ** -0.5, ALU.add, ALU.mult).then_inc(s_setup_v, 1)
            dve.wait_ge(s_setup_v, 3)
            v.tensor_copy(khi[:, :, :], krep[:, :, :]).then_inc(s_setup_v, 1)
            dve.wait_ge(s_setup_pe, 3)
            dve.wait_ge(s_setup_v, 4)
            v.tensor_tensor(klo[:, :, :], krep[:, :, :], khi[:, :, :].bitcast(F32), ALU.subtract)
            v.tensor_tensor(vall[:, :, :], ps[:, 2, 0:B * DK].rearrange("p (b d) -> p b d", b=B),
                            bvs[:, :].rearrange("p (b d) -> p b d", b=1).broadcast_to([P, B, DK]),
                            ALU.add).then_inc(s_setup_v, 1)

            def wq_lo():
                dve.wait_ge(s_wqh, 1)
                v.tensor_tensor(wql[:, :, :], wq32, wqh[:, :, :].bitcast(F32), ALU.subtract).then_inc(s_wql, 1)

            def w1_lo():
                dve.wait_ge(s_w1h, 1)
                v.tensor_tensor(w1l[:, :, :], w1_32, w1h[:, :, :].bitcast(F32), ALU.subtract).then_inc(s_w1l, 1)

            def stats(src, ln, sems, count):
                st, su, dm, mu, va, vb, ve, _ = ln
                s_stats, s_halves, s_parts, s_var = sems
                for k in range(NT):
                    a = v.bn_stats(st[:, k].rearrange("p a c -> p (a c)"), src(k))
                a.then_inc(s_stats, 1)
                dve.wait_ge(s_stats, count)
                v.tensor_tensor(su[:, :, :], st[:, :, 0, :], st[:, :, 1, :], ALU.add)
                v.tensor_tensor(dm[:, :], st[:, :, 0, 1], st[:, :, 1, 1], ALU.subtract).then_inc(s_halves, 1)
                dve.wait_ge(s_halves, count)
                v.tensor_scalar(mu[:, :], su[:, :, 1], 0.5, None, ALU.mult)
                v.tensor_scalar(va[:, :], su[:, :, 2], 1.0 / D, EPS, ALU.mult, ALU.add)
                v.scalar_tensor_tensor(out=vb[:, :], in0=dm[:, :], scalar=0.25, in1=dm[:, :],
                                       op0=ALU.mult, op1=ALU.mult).then_inc(s_parts, 1)
                dve.wait_ge(s_parts, count)
                v.tensor_tensor(ve[:, :], va[:, :], vb[:, :], ALU.add).then_inc(s_var, 1)

            def normalise(dst, src, ln, s_r, s_done, count):
                dve.wait_ge(s_r, count)
                for k in range(NT):
                    a = v.tensor_scalar(dst(k), src(k), ln[3][:, k:k + 1], ln[7][:, k:k + 1], ALU.subtract, ALU.mult)
                a.then_inc(s_done, 1)

            def layernorm1(b, j):
                c = at(b, NJ, j + 1)
                dve.wait_ge(s_x[j], at(b, 16, 16))
                stats(lambda k: xin[:, j, k, :], ln1, (s_ln1s, s_ln1h, s_ln1p, s_ln1v), c)
                dve.wait_ge(s_m[j], at(b, 16, 16))
                dve.wait_ge(s_mTp, at(b, NJ, j))
                v.tensor_scalar(mb[:, :, :, :], min_[:, j].rearrange("p k (a s) -> p k a s", a=1).broadcast_to([P, NT, 2, SK]),
                                0, MASKED, ALU.is_equal, ALU.mult).then_inc(s_mb, 1)
                dve.wait_ge(s_xTp, at(b, NJ, j))
                normalise(lambda k: xh1[:, k, :], lambda k: xin[:, j, k, :], ln1, s_ln1r, s_ln1, c)

            def x_lo(b, j):
                dve.wait_ge(s_qp, at(b, NJ * KD, j * KD))
                for c in range(KD):
                    dve.wait_ge(s_xTh, at(b, NJ * KD, j * KD + c + 1))
                    a = v.tensor_tensor(xTl[:, c, :], ps[:, c, :], xTh[:, c, :].bitcast(F32), ALU.subtract)
                a.then_inc(s_xTl, 1)

            def q_lo(b, j):
                dve.wait_ge(s_qh, at(b, NJ, j + 1))
                for m in range(KD):
                    for par in range(2):
                        r, _ = halves(par)
                        a = v.scalar_tensor_tensor(out=ql[r, 2 * m + par, :], in0=ps[r, m, :], scalar=bqs[r, m:m + 1],
                                                   in1=qh[r, 2 * m + par, :].bitcast(F32), op0=ALU.add, op1=ALU.subtract)
                a.then_inc(s_ql, 1)

            def take_max(b, j):
                dve.wait_ge(s_nTp, at(b, NJ, j))
                for k in range(NT):
                    dve.wait_ge(s_sn, at(b, NJ * NT, j * NT + k + 1))
                    bank = 2 + 2 * (k % 2)
                    v.tensor_reduce(mx[:, k, :].rearrange("p (a h) -> p a h", a=2),
                                    ps[:, bank:bank + 2, :].rearrange("p a (h s) -> p a h s", s=SK),
                                    AX.X, ALU.max).then_inc(s_mx, 1)
                dve.wait_ge(s_mx, at(b, NJ * NT, (j + 1) * NT))
                v.tensor_scalar(nm[:, :, 0:H], mx[:, :, :], -1.0, None, ALU.mult).then_inc(s_nmh, 1)
                dve.wait_ge(s_nmh, at(b, NJ, j + 1))
                v.scalar_tensor_tensor(out=nm[:, :, H:2 * H], in0=mx[:, :, :], scalar=-1.0,
                                       in1=nm[:, :, 0:H].bitcast(F32), op0=ALU.mult, op1=ALU.subtract).then_inc(s_nm, 1)

            def invert(b, j):
                dve.wait_ge(s_dn, at(b, NJ, j + 1))
                v.reciprocal(rD[:, :], ps[:, 2, 0:P]).then_inc(s_rd, 1)

            def attn_normalise(b, j):
                dve.wait_ge(s_bc, at(b, NJ, j + 1))
                dve.wait_ge(s_osb, at(b, NJ, j + 1))
                v.tensor_tensor(oT[:, :, :], osb[:, :, :], ps[:, 4:6, :], ALU.mult).then_inc(s_oT, 1)

            def x1_ln2(b, j):
                c = at(b, NJ, j + 1)
                dve.wait_ge(s_wo, c)
                dve.wait_ge(s_xb, c)
                v.tensor_tensor(x1[:, j].rearrange("p (a k) d -> p a (k d)", a=2), ps[:, 0:2, :],
                                xb[:, j].rearrange("p (a k) d -> p a (k d)", a=2), ALU.add).then_inc(s_x1, 1)
                dve.wait_ge(s_x1, c)
                stats(lambda k: x1[:, j, k, :], ln2, (s_ln2s, s_ln2h, s_ln2p, s_ln2v), c)
                normalise(lambda k: xh2[:, j, k, :], lambda k: x1[:, j, k, :], ln2, s_ln2r, s_ln2, c)

            def mix(b, j):
                dve.wait_ge(s_x2T, at(b, NJ, NJ))
                for c in range(KD):
                    n = at(b, NJ * KD, j * KD + c + 1)
                    t = j * CH
                    if j > 0:
                        dve.wait_ge(s_xml, at(b, NJ * KD, (j - 1) * KD + c + 1))
                        dve.wait_ge(s_xmh, at(b, NJ * KD, (j - 1) * KD + c + 1))
                    v.tensor_scalar(xm[:, c, :], x2T[:, c, t:t + CH], mks[:, 0, c:c + 1], None, ALU.mult).then_inc(s_mix1, 1)
                    dve.wait_ge(s_mix1, n)
                    v.scalar_tensor_tensor(out=xm[:, c, :], in0=x2T[:, c, t + 1:t + 1 + CH], scalar=mks[:, 1, c:c + 1],
                                           in1=xm[:, c, :], op0=ALU.mult, op1=ALU.add).then_inc(s_mix2, 1)
                    dve.wait_ge(s_mix2, n)
                    v.scalar_tensor_tensor(out=xm[:, c, :], in0=x2T[:, c, t + 2:t + 2 + CH], scalar=mks[:, 2, c:c + 1],
                                           in1=xm[:, c, :], op0=ALU.mult, op1=ALU.add).then_inc(s_xm, 1)

            def argmax(b, j):
                n, bank = slot(j, "gate")
                c = at(b, NJ, j + 1)
                dve.wait_ge(s_f, at(b, NJ * NU, n + 1))
                v.tensor_tensor(gs[:, :, :], ps[:, bank, 0:NT * NPATH].rearrange("p (k n) -> p k n", n=NPATH),
                                bo2s[:, :].rearrange("p (k n) -> p k n", k=1).broadcast_to([P, NT, NPATH]),
                                ALU.add).then_inc(s_fv, 1)
                dve.wait_ge(s_fv, 1 + at(b, NJ * NFV, j * NFV + 1))
                v.tensor_reduce(gmax[:, :], gs[:, :, :], AX.X, ALU.max).then_inc(s_g2, 1)
                dve.wait_ge(s_g2, c)
                iota = cst[:, C_IO:C_IO + NPATH].rearrange("p (k n) -> p k n", k=1).broadcast_to([P, NT, NPATH])

                def per_tile(t):
                    return t[:, :].rearrange("p (k n) -> p k n", n=1).broadcast_to([P, NT, NPATH])

                v.tensor_tensor(cand[:, :, :], gs[:, :, :], per_tile(gmax), ALU.is_ge).then_inc(s_g3, 1)
                dve.wait_ge(s_g3, at(b, 2 * NJ, 2 * j + 1))
                v.tensor_tensor(gs[:, :, :], cand[:, :, :], iota, ALU.mult).then_inc(s_g3, 1)
                dve.wait_ge(s_g3, at(b, 2 * NJ, 2 * j + 2))
                v.tensor_reduce(gidx[:, :], gs[:, :, :], AX.X, ALU.min).then_inc(s_g4, 1)
                dve.wait_ge(s_g4, c)
                v.tensor_tensor(oh[:, :, 0:NPATH], iota, per_tile(gidx), ALU.is_equal).then_inc(s_oh, 1)

            def select(b, j):
                dve.wait_ge(s_fa, at(b, NJ * NFA, (j + 1) * NFA))
                for m in range(NM):
                    n, bank = slot(j, f"rep{m}")
                    r = P if m < 4 else DM + NPATH
                    dve.wait_ge(s_f, at(b, NJ * NU, n + 1))
                    dst = hs[:, m, :] if m < 4 else h4s[0:r, :]
                    v.tensor_tensor(dst, hs[0:r, m, :], ps[0:r, bank, :], ALU.mult).then_inc(s_fv, 1)

            def residual_ln3(b, j):
                c = at(b, NJ, j + 1)
                dve.wait_ge(s_yg, 1 + at(b, NJ, j))
                for i, u in enumerate(("w2a", "w2b")):
                    n, bank = slot(j, u)
                    dve.wait_ge(s_f, at(b, NJ * NU, n + 1))
                    v.tensor_tensor(res[:, 2 * i:2 * i + 2, :], xh2[:, j, 2 * i:2 * i + 2, :],
                                    ps[:, bank, :].rearrange("p (k d) -> p k d", d=D), ALU.add).then_inc(s_fv, 1)
                dve.wait_ge(s_fv, 1 + at(b, NJ * NFV, (j + 1) * NFV))
                stats(lambda k: res[:, k, :], ln3, (s_ln3s, s_ln3h, s_ln3p, s_ln3v), c)
                normalise(lambda k: res[:, k, :], lambda k: res[:, k, :], ln3, s_ln3r, s_ln3, c)

            def step(ba, bf, last=False):
                if bf is not None:
                    for j in range(NJ):
                        mix(bf, j)
                for j in range(NJ):
                    if ba is not None:
                        layernorm1(ba, j)
                        x_lo(ba, j)
                        q_lo(ba, j)
                    if bf is not None:
                        argmax(bf, j)
                    if ba is not None:
                        take_max(ba, j)
                    if bf is not None:
                        select(bf, j)
                        residual_ln3(bf, j)
                    if ba is not None:
                        invert(ba, j)
                        attn_normalise(ba, j)
                        if bf is not None:
                            dve.wait_ge(s_x1b, at(bf, NJ, j + 1))
                        x1_ln2(ba, j)

            wq_lo()
            w1_lo()
            step(0, None)
            with dve.Fori(1, B) as b:
                step(b, b - 1)
            step(None, B - 1)

        @block.gpsimd
        def _(pool):
            g = nc.gpsimd
            g.memset(halfneg[:, :], -0.5).then_inc(s_init, 1)
            g.memset(unused[:, 0:1], 0.0).then_inc(s_yg, 1)
            g.memset(unused[:, 1:2], 0.0).then_inc(s_yo, 1)
            g.memset(unused[:, 2:3], 0.0).then_inc(s_out[1], 16)
            pool.wait_ge(s_init, 2)
            pool.wait_ge(s_setup_v, 5)

            def operands(b):
                pool.wait_ge(s_dn, at(b, NJ, 0))

                def keys(src, rows):
                    k = src[rows, bass.ds(b, 1), :]
                    return k.broadcast_to([64, 4, SK])

                def d4(rows):
                    return cst[rows, C_D4:C_D4 + 256].rearrange("p (h s) -> p h s", h=4)

                def to(dst, rows, i):
                    return dst[rows, i, :].rearrange("p (h s) -> p h s", h=4)

                for par in range(2):
                    r, _ = halves(par)
                    g.tensor_tensor(to(kmh, r, par), keys(khi[:, :, :].bitcast(F32), r), d4(r), ALU.mult)
                    g.tensor_tensor(to(kml, r, par), keys(klo, r), d4(r), ALU.mult)
                    for q in (par, par + 2):
                        a = g.tensor_tensor(to(kms, r, q), keys(khi[:, :, :].bitcast(F32), r), d4(r), ALU.mult)
                    a.then_inc(s_km, 1)
                    pool.wait_ge(s_km, at(b, 3, par + 1))
                g.tensor_tensor(vd[:, :].rearrange("p (h d) -> p h d", h=2), vall[:, bass.ds(b, 1), :].broadcast_to([P, 2, DK]),
                                cst[:, C_VM:C_VM + 32].rearrange("p (h d) -> p h d", h=2), ALU.mult).then_inc(s_km, 1)

            def rstd(ln, s_v, s_r, c):
                pool.wait_ge(s_v, c)
                g.tensor_tensor(ln[7][:, :], ln[6][:, :], halfneg[:, :], ALU.pow).then_inc(s_r, 1)

            def add_bo(b, j):
                pool.wait_ge(s_x1, at(b, NJ, j))
                pool.wait_ge(s_x[j], at(b, 16, 16))
                g.tensor_tensor(xb[:, j], xin[:, j], bos[:, :].rearrange("p (k d) -> p k d", k=1).broadcast_to([P, NT, D]),
                                ALU.add).then_inc(s_xb, 1)

            def add_beta(b, j):
                pool.wait_ge(s_yo, 1 + at(b, NJ, j))
                g.tensor_tensor(x1b[:, :, :], x1[:, j], bts[:, :].rearrange("p (k d) -> p k d", k=1).broadcast_to([P, NT, D]),
                                ALU.add).then_inc(s_x1b, 1)

            def mixed_lo(b, j):
                for c in range(KD):
                    pool.wait_ge(s_xmh, at(b, NJ * KD, j * KD + c + 1))
                    js = slice(j * CH, (j + 1) * CH)
                    g.tensor_tensor(xml[:, c, js], xm[:, c, :], xmh[:, c, js].bitcast(F32), ALU.subtract).then_inc(s_xml, 1)

            def finish(b, j):
                c = at(b, NJ, j + 1)
                pool.wait_ge(s_ln3, c)
                if j == 0:
                    pool.wait_ge(s_out[1], at(b, 16, 16))
                else:
                    pool.wait_ge(s_out[0], at(b, 16, 16))
                g.tensor_tensor(y[:, :, :], res[:, :, :], gms[:, :].rearrange("p (k d) -> p k d", k=1).broadcast_to([P, NT, D]),
                                ALU.mult).then_inc(s_yg, 1)
                pool.wait_ge(s_yg, 1 + c)
                pool.wait_ge(s_x1b, c)
                g.tensor_tensor(y[:, :, :], y[:, :, :], x1b[:, :, :], ALU.add).then_inc(s_yo, 1)

            def step(ba, bf):
                if bf is not None:
                    for j in range(NJ):
                        mixed_lo(bf, j)
                if ba is not None:
                    operands(ba)
                for j in range(NJ):
                    if ba is not None:
                        rstd(ln1, s_ln1v, s_ln1r, at(ba, NJ, j + 1))
                        add_bo(ba, j)
                    if bf is not None:
                        add_beta(bf, j)
                        rstd(ln3, s_ln3v, s_ln3r, at(bf, NJ, j + 1))
                        finish(bf, j)
                    if ba is not None:
                        rstd(ln2, s_ln2v, s_ln2r, at(ba, NJ, j + 1))

            pool.wait_ge(s_wf, 16 * WF_LOADS)
            pool.wait_ge(s_wa, 16 * WA_LOADS)
            step(0, None)
            with pool.Fori(1, B) as b:
                step(b, b - 1)
            step(None, B - 1)


WA_LOADS = 5 + P // DK + 3
WF_LOADS = NPATH + 1 + 4 + 3 + 4

_PREFIX = ("L0_xattn_", "L0_ffn_")
_ATTN = ["Wq", "bq", "Wk", "bk", "Wv", "bv", "Wo", "bo"]
_FFN = ["mix_kernel", "W1", "b1", "W2", "b2", "Wo1", "bo1", "Wo2", "bo2", "gamma", "beta"]


def kernel(**inputs):
    from concourse import bacc
    from concourse.bass_utils import run_bass_kernel_spmd

    nc = bacc.Bacc("TRN2", target_bir_lowering=False, num_devices=1)
    names = ["x", "ctx_1024", "mask_Bx1xSxS2_ik1"] + [_PREFIX[0] + n for n in _ATTN] + [_PREFIX[1] + n for n in _FFN]
    arrays = {n: np.ascontiguousarray(inputs[n]) for n in names}
    arrays["constants"] = constants()
    args = [nc.dram_tensor(f"in_{n}", a.shape, mybir.dt.from_np(a.dtype), kind="ExternalInput").ap()
            for n, a in arrays.items()]
    out = nc.dram_tensor("out_0", (B, S, D), F32, kind="ExternalOutput").ap()
    layer_program(nc, *args, out)
    r = run_bass_kernel_spmd(nc, [{f"in_{n}": a for n, a in arrays.items()}], core_ids=[0])
    return r.results[0]["out_0"]
```

```python
from contextlib import ExitStack

import numpy as np

import concourse.bass as bass
from concourse import mybir

F32 = mybir.dt.float32
F32R = mybir.dt.float32r
BF16 = mybir.dt.bfloat16
I32 = mybir.dt.int32
ALU = mybir.AluOpType
ACT = mybir.ActivationFunctionType
AX = mybir.AxisListType

P = 128
B, S, D = 4, 1024, 256
SK = 64
H, DK = 16, 16
NPATH, DM = 9, 64
CH = 512
NJ = S // CH
NT = CH // P
KD = D // P
NQ = 4
NPAIR = H // 2
NM = 5
EPS = 1e-5
MASKED = -float(2.0 ** 100)

C_ID = 0
C_D4 = C_ID + P
C_IDK = C_D4 + 4 * SK
C_SEL = C_IDK + 4 * SK
C_E = C_SEL + NQ * 4 * SK
C_BC = C_E + NPAIR * 32
C_VM = C_BC + KD * NT * P
C_IO = C_VM + 32
C_N = C_IO + NPATH


def constants():
    c = np.zeros((P, C_N), np.float32)
    r = np.arange(P)[:, None]
    hk = np.arange(4 * SK)[None, :]
    c[:, C_ID:C_ID + P] = np.eye(P)
    c[:, C_D4:C_D4 + 4 * SK] = (r % 64) // DK == hk // SK
    c[:, C_IDK:C_IDK + 4 * SK] = r % 64 == hk % SK
    for q in range(NQ):
        c[:, C_SEL + q * 4 * SK:C_SEL + (q + 1) * 4 * SK] = (r % 64 < 32) & (r % 16 == 4 * q + hk // SK)
    for p in range(NPAIR):
        c[:, C_E + 32 * p:C_E + 32 * p + 32] = np.arange(32)[None, :] % 16 == 2 * p + r // 64
    for m in range(KD):
        for k in range(NT):
            at = C_BC + P * (m * NT + k)
            c[:, at:at + P] = r == 32 * k + 8 * m + np.arange(P)[None, :] // DK
    c[:, C_VM:C_VM + 32] = r // 64 == np.arange(32)[None, :] // DK
    c[:, C_IO:C_IO + NPATH] = np.arange(NPATH) - NPATH
    return c


def layer_program(nc, x, ctx, mask, Wq, bq, Wk, bk, Wv, bv, Wo, bo, mixk, W1, b1, W2, b2,
                  Wo1, bo1, Wo2, bo2, gamma, beta, consts, out):
    with ExitStack() as stack:
        def sb(name, shape, dt=F32):
            return stack.enter_context(nc.sbuf_tensor(name, shape, dt))

        def sem(name):
            return stack.enter_context(nc.semaphore(name))

        stack.enter_context(nc.allow_non_contiguous_dma("biases, one value per partition"))

        cst = sb("cst", [P, C_N])
        ident_b = sb("ident_b", [P, P], BF16)
        wqh, wql = sb("wqh", [P, KD, D], F32R), sb("wql", [P, KD, D], F32R)
        w1h, w1l = sb("w1h", [P, KD, NM * P], F32R), sb("w1l", [P, KD, NM * P], F32R)
        w2h, w2l = sb("w2h", [P, NM, D], F32R), sb("w2l", [P, NM, D], F32R)
        wo = sb("wo", [P, KD, D])
        wo2 = sb("wo2", [P, NPATH])
        wk = sb("wk", [P, KD, DK])
        wk8 = sb("wk8", [P, KD, P])
        wv = sb("wv", [P, KD, DK])
        bqs = sb("bqs", [P, KD])
        bks = sb("bks", [P, 1])
        bvs = sb("bvs", [P, DK])
        bos, gms, bts = sb("bos", [P, D]), sb("gms", [P, D]), sb("bts", [P, D])
        b1s = sb("b1s", [P, NM])
        bo2s = sb("bo2s", [P, NPATH])
        mks = sb("mks", [P, 3, KD])
        unused = sb("unused", [P, 4])
        halfneg = sb("halfneg", [P, NT])
        khi = sb("khi", [P, B, SK], F32R)
        klo = sb("klo", [P, B, SK])
        krep = sb("krep", [P, B, SK])
        vall = sb("vall", [P, B, DK])
        kmh = sb("kmh", [P, 2, 4 * SK], F32R)
        kml = sb("kml", [P, 2, 4 * SK], F32R)
        kms = sb("kms", [P, NQ, 4 * SK], F32R)
        vd = sb("vd", [P, 2 * DK])
        def ln_buffers(n):
            return (sb(f"st{n}", [P, NT, 2, 3]), sb(f"su{n}", [P, NT, 3]), sb(f"dm{n}", [P, NT]), sb(f"mu{n}", [P, NT]),
                    sb(f"va{n}", [P, NT]), sb(f"vb{n}", [P, NT]), sb(f"ve{n}", [P, NT]), sb(f"rs{n}", [P, NT]))

        xin = sb("xin", [P, NJ, NT, D])
        min_ = sb("min_", [P, NJ, NT, SK], I32)
        mb = sb("mb", [P, NT, 2, SK], BF16)
        mT = sb("mT", [P, CH])
        ln1 = ln_buffers("1")
        ln2 = ln_buffers("2")
        ln3 = ln_buffers("3")
        xh1 = sb("xh1", [P, NT, D])
        xTh, xTl = sb("xTh", [P, KD, CH], F32R), sb("xTl", [P, KD, CH], F32R)
        qh = sb("qh", [P, NQ, CH], F32R)
        ql = sb("ql", [P, NQ, CH], F32R)
        mx = sb("mx", [P, NT, H])
        nm = sb("nm", [P, NT, 2 * H], F32R)
        e = sb("e", [P, NPAIR, CH])
        ctx_in = e[0:SK, 0:2, :].rearrange("p a (b d) -> p (a b) d", d=D)
        ctxT = e[:, 2:4, :].rearrange("p c (b a s) -> p c b a s", b=B, a=2)
        rD = sb("rD", [P, P])
        osb = sb("osb", [P, KD, CH])
        x1 = sb("x1", [P, NJ, NT, D])
        xh2 = sb("xh2", [P, NJ, NT, D])
        x2T = sb("x2T", [P, KD, S + 2])
        xm = sb("xm", [P, KD, CH])
        xmh, xml = sb("xmh", [P, KD, S], F32R), sb("xml", [P, KD, S], F32R)
        hs = sb("hs", [P, NM, CH])
        h4s = sb("h4s", [P, CH])
        hmh, hml = sb("hmh", [P, NM, CH], F32R), sb("hml", [P, NM, CH], F32R)
        wq32 = h4s[:, :].rearrange("p (c n) -> p c n", c=KD)
        hs_flat = hs[:, :, :].rearrange("p m t -> p (m t)")
        w1_32 = hs_flat[:, 0:KD * NM * P].rearrange("p (c n) -> p c n", c=KD)
        w2_32 = hs_flat[:, KD * NM * P:KD * NM * P + NM * D].rearrange("p (m n) -> p m n", m=NM)
        thT = sb("thT", [P, CH])
        nmT = thT[0:32, :]
        gs = sb("gs", [P, NT, NPATH])
        gmax = sb("gmax", [P, NT])
        cand = sb("cand", [P, NT, NPATH])
        gidx = sb("gidx", [P, NT])
        oh = sb("oh", [P, NT, NPATH + 1], BF16)
        x1b = sb("x1b", [P, NT, D])
        xh2f = sb("xh2f", [P, NT, D])
        y = sb("y", [P, NT, D])

        ps = stack.enter_context(nc.psum_tensor("ps", [P, 8, CH], F32))

        ident = cst[:, C_ID:C_ID + P]
        ps_b = ps[:, 2, 0:CH // 2].bitcast(BF16)

        s_cst, s_wa, s_wf = sem("consts_loaded"), sem("attn_weights_loaded"), sem("ffn_weights_loaded")
        s_x = [sem(f"x_loaded{j}") for j in range(NJ)]
        s_m = [sem(f"mask_loaded{j}") for j in range(NJ)]
        s_init = sem("memsets_done")
        s_wqh, s_wql, s_w1h, s_w1l = sem("wq_hi"), sem("wq_lo"), sem("w1_hi"), sem("w1_lo")
        s_w2h, s_w2l, s_ones = sem("w2_hi"), sem("w2_lo"), sem("b2_selector_ones")
        s_id = sem("identity_in_bf16")
        s_setup_pe, s_setup_v = sem("setup_products"), sem("setup_copies")
        s_km = sem("score_operands_built")
        s_ln1s, s_ln1h, s_ln1p = sem("ln1_stats"), sem("ln1_halves"), sem("ln1_var_parts")
        s_ln1v, s_ln1r, s_ln1 = sem("ln1_var"), sem("ln1_rstd"), sem("ln1_done")
        s_ln2s, s_ln2h, s_ln2p = sem("ln2_stats"), sem("ln2_halves"), sem("ln2_var_parts")
        s_ln2v, s_ln2r, s_ln2 = sem("ln2_var"), sem("ln2_rstd"), sem("ln2_done")
        s_ln3s, s_ln3h, s_ln3p = sem("ln3_stats"), sem("ln3_halves"), sem("ln3_var_parts")
        s_ln3v, s_ln3r, s_ln3 = sem("ln3_var"), sem("ln3_rstd"), sem("ln3_done")
        s_mb, s_xb = sem("mask_bias"), sem("x_plus_bo")
        s_mTp, s_mT = sem("maskT_in_psum"), sem("maskT_copied")
        s_mrow = sem("mask_rows_placed")
        s_xTp, s_xTh, s_xTl = sem("xT_in_psum"), sem("xT_hi"), sem("xT_lo")
        s_qp, s_qh, s_ql = sem("q_in_psum"), sem("q_hi"), sem("q_lo")
        s_sn, s_mx = sem("scores_for_max"), sem("max_taken")
        s_nmh, s_nm = sem("negmax_hi"), sem("negmax_split")
        s_nTp, s_nT, s_nrow = sem("negmaxT_in_psum"), sem("negmaxT_copied"), sem("negmax_rows_placed")
        s_st, s_e = sem("scoresT_in_psum"), sem("exp_done")
        s_o, s_dn, s_osb = sem("pv_in_psum"), sem("denominators_in_psum"), sem("pv_copied")
        s_rd, s_bc, s_oT = sem("denominators_inverted"), sem("inverse_spread"), sem("attn_normalised")
        s_wo, s_x1 = sem("wo_in_psum"), sem("x1_done")
        s_x2p, s_x2T = sem("x2T_in_psum"), sem("x2T_copied")
        s_mix1, s_mix2, s_xm = sem("mix_one_term"), sem("mix_two_terms"), sem("mixed")
        s_xmh, s_xml = sem("mixed_hi"), sem("mixed_lo")
        s_f, s_fa, s_fv = sem("ffn_slot_filled"), sem("ffn_slot_read_by_act"), sem("ffn_slot_read_by_dve")
        s_g1, s_g2, s_g3, s_g4, s_oh = sem("gate_scores"), sem("gate_max"), sem("gate_cand"), sem("gate_index"), sem("onehot")
        s_res, s_x1b, s_yg, s_yo = sem("ffn_residual"), sem("x1_plus_beta"), sem("times_gamma"), sem("out_ready")
        s_xh2f, s_sel, s_hh, s_hl = sem("xh2_kept"), sem("path_selected"), sem("selected_hi"), sem("selected_lo")
        s_out = [sem(f"out_stored{j}") for j in range(NJ)]

        def at(b, per_row, n):
            return b * per_row + n

        xr = x.rearrange("b (j k p) d -> p b j k d", p=P, k=NT)
        outr = out.rearrange("b (j k p) d -> p b j k d", p=P, k=NT)
        mr = mask.rearrange("b o (j k p) s -> p (b o) j k s", p=P, k=NT)

        def halves(par):
            return (slice(0, 64), slice(64, 128)) if par == 0 else (slice(64, 128), slice(0, 64))

        def row_broadcast(vec, n, parts=P):
            return vec.rearrange("(o n) -> o n", o=1).broadcast_to([parts, n])

        USES = ["h4", "gate", "h0", "h1", "h2", "h3", "rep0", "rep1", "rep2", "rep3", "rep4", "w2a", "w2b"]
        NU = len(USES)
        BY_ACT = [u in ("h4", "h0", "h1", "h2", "h3") for u in USES]
        NFA, NFV = sum(BY_ACT), NU - sum(BY_ACT)

        def slot(j, u):
            n = j * NU + USES.index(u)
            return n, 6 + n % 2

        def reads_before(n, by_act):
            return sum(BY_ACT[i % NU] == by_act for i in range(n))

        block = stack.enter_context(nc.Block())

        @block.sync
        def _(sp):
            def load(dst, src, s):
                sp.dma_start(dst, src).then_inc(s, 16)

            load(cst[:, :], consts, s_cst)
            load(xin[:, 0], xr[:, 0, 0], s_x[0])
            load(min_[:, 0], mr[:, 0, 0], s_m[0])
            load(ctx_in, ctx.rearrange("b s d -> s b d"), s_wa)
            load(wk[:, :, :], Wk.rearrange("(c p) n -> p c n", p=P), s_wa)
            load(wv[:, :, :], Wv.rearrange("(c p) n -> p c n", p=P), s_wa)
            load(wq32, Wq.rearrange("(c p) n -> p c n", p=P), s_wa)
            load(bqs[:, :], bq.rearrange("(c p) -> p c", p=P), s_wa)
            for h in range(P // DK):
                load(bks[h * DK:(h + 1) * DK, :], bk.rearrange("(p o) -> p o", o=1), s_wa)
            load(bvs[:, :], row_broadcast(bv, DK), s_wa)
            load(bos[:, :], row_broadcast(bo, D), s_wa)
            load(wo[:, :, :], Wo.rearrange("(c p) n -> p c n", p=P), s_wa)
            load(xin[:, 1], xr[:, 0, 1], s_x[1])
            load(min_[:, 1], mr[:, 0, 1], s_m[1])
            for p in range(NPATH):
                load(w1_32[:, :, p * DM:(p + 1) * DM], W1[p].rearrange("(c p) m -> p c m", p=P), s_wf)
            load(w1_32[:, :, NPATH * DM:], Wo1.rearrange("(c p) m -> p c m", p=P), s_wf)
            load(w2_32[:, 0:4, :], W2[0:8].rearrange("(t a) m d -> (a m) t d", a=2), s_wf)
            load(w2_32[0:DM, 4, :], W2[8], s_wf)
            load(w2_32[DM:DM + NPATH, 4, :], b2, s_wf)
            load(wo2[DM:, :], Wo2, s_wf)
            load(b1s[:, 0:4], b1[0:8].rearrange("(t a) m -> (a m) t", a=2), s_wf)
            load(b1s[0:DM, 4:5], b1[8].rearrange("(m o) -> m o", o=1), s_wf)
            load(b1s[DM:, 4:5], bo1.rearrange("(m o) -> m o", o=1), s_wf)
            load(bo2s[:, :], row_broadcast(bo2, NPATH), s_wf)
            load(mks[:, :, :], mixk.rearrange("t (c p) -> p t c", p=P), s_wf)
            load(gms[:, :], row_broadcast(gamma, D), s_wf)
            load(bts[:, :], row_broadcast(beta, D), s_wf)

            def place_mask(b, j):
                sp.wait_ge(s_st, at(b, NJ * NPAIR, j * NPAIR))
                sp.wait_ge(s_mT, at(b, NJ, j + 1))
                for par in range(2):
                    _, mrow = halves(par)
                    for q in (par, par + 2):
                        sp.dma_start(qh[mrow, q, :].bitcast(F32), mT[mrow, :]).then_inc(s_mrow, 16)

            def place_maxima(b, j):
                sp.wait_ge(s_nT, at(b, NJ, j + 1))
                for par in range(2):
                    r0 = halves(par)[1].start
                    for q in (par, par + 2):
                        sp.dma_start(ql[r0:r0 + 32, q, :].bitcast(F32), nmT).then_inc(s_nrow, 16)

            def next_inputs(b, j):
                sp.wait_ge(s_ln1, at(b, NJ, j + 1))
                sp.wait_ge(s_xb, at(b, NJ, j + 1))
                sp.dma_start(xin[:, j], xr[:, b + 1, j]).then_inc(s_x[j], 16)
                sp.wait_ge(s_mb, at(b, NJ, j + 1))
                sp.dma_start(min_[:, j], mr[:, b + 1, j]).then_inc(s_m[j], 16)

            def store(b, j):
                sp.wait_ge(s_yo, 1 + at(b, NJ, j + 1))
                sp.dma_start(outr[:, b, j], y[:, :, :]).then_inc(s_out[j], 16)

            def row(r, feed_forward, more):
                for j in range(NJ):
                    front = (r, 1) if j == 0 else (r + 1, 0)
                    if j == 0 or more:
                        place_mask(*front)
                    if more:
                        next_inputs(r, j)
                    if j == 0 or more:
                        place_maxima(*front)
                    if feed_forward:
                        store(r - 1, j)

            place_mask(0, 0)
            place_maxima(0, 0)
            row(0, False, True)
            with sp.Fori(1, B - 1) as r:
                row(r, True, True)
            row(B - 1, True, False)
            for j in range(NJ):
                store(B - 1, j)
            for j in range(NJ):
                sp.wait_ge(s_out[j], 16 * B + (16 if j == NJ - 1 else 0))

        @block.tensor
        def _(pe):
            def three_pass(out_, lhs, rhs, more):
                terms = [(lhs[0], rhs[0]), (lhs[0], rhs[1]), (lhs[1], rhs[0])]
                n = 0
                for a, c in terms:
                    for k in range(KD):
                        n += 1
                        mm = nc.tensor.matmul(out_, a(k), c(k), start=(n == 1),
                                              stop=(n == 3 * KD and not more))
                return mm

            pe.wait_ge(s_cst, 16)
            pe.wait_ge(s_wa, 16 * WA_LOADS)
            for b in range(B):
                for k in range(KD):
                    i = (k * B + b) * SK
                    mm = nc.tensor.transpose(ps[:, 0, i:i + SK], ctx_in[:, b, k * P:(k + 1) * P], ident[0:SK, 0:SK])
            mm.then_inc(s_setup_pe, 1)
            pe.wait_ge(s_setup_v, 2)
            for k in range(KD):
                mm = nc.tensor.matmul(ps[:, 1, 0:B * SK].rearrange("p (b s) -> p b s", b=B), wk8[:, k, :],
                                      ctxT[:, k, :, 0, :], start=(k == 0), stop=(k == KD - 1))
            mm.then_inc(s_setup_pe, 1)
            for b in range(B):
                for k in range(KD):
                    mm = nc.tensor.matmul(ps[:, 2, b * DK:(b + 1) * DK], ctxT[:, k, b, :, :], wv[:, k, :],
                                          start=(k == 0), stop=(k == KD - 1))
            mm.then_inc(s_setup_pe, 1)

            def t1(b, j):
                pe.wait_ge(s_mb, at(b, NJ, j + 1))
                pe.wait_ge(s_mx, at(b, NJ * NT, j * NT))
                for k in range(NT):
                    mm = nc.tensor.transpose(ps_b[:, k * P:(k + 1) * P], mb[:, k, :, :], ident_b[:, :])
                mm.then_inc(s_mTp, 1)
                pe.wait_ge(s_ln1, at(b, NJ, j + 1))
                pe.wait_ge(s_nT, at(b, NJ, j))
                if j > 0 or not isinstance(b, int) or b > 0:
                    pe.wait_ge(s_x2T, at(b, NJ, j - 1))
                for c in range(KD):
                    for k in range(NT):
                        mm = nc.tensor.transpose(ps[:, c, k * P:(k + 1) * P], xh1[:, k, c * P:(c + 1) * P], ident)
                mm.then_inc(s_xTp, 1)

            def wq(b, j):
                pe.wait_ge(s_xTl, at(b, NJ, j + 1))
                for m in range(KD):
                    ms = slice(m * P, (m + 1) * P)
                    mm = three_pass(ps[:, m, :], (lambda k: wqh[:, k, ms], lambda k: wql[:, k, ms]),
                                    (lambda k: xTh[:, k, :], lambda k: xTl[:, k, :]), False)
                    mm.then_inc(s_qp, 1)

            def scores_for_max(b, j, tiles):
                if tiles[0] > 0:
                    for k in tiles:
                        max_tile(b, j, k)
                    return
                pe.wait_ge(s_qh, at(b, NJ, j + 1))
                pe.wait_ge(s_mrow, at(b, 16 * NJ * NQ, (j + 1) * NQ * 16))
                pe.wait_ge(s_km, at(b, 3, 3))
                pe.wait_ge(s_oT, at(b, NJ, j))
                pe.wait_ge(s_mT, at(b, NJ, j + 1))
                for k in tiles:
                    max_tile(b, j, k)

            def max_tile(b, j, k):
                if k >= 2:
                    pe.wait_ge(s_mx, at(b, NJ * NT, j * NT + k - 1))
                for q in range(NQ):
                    bank = 2 + 2 * (k % 2) + q // 2
                    mm = nc.tensor.matmul(ps[:, bank, (q % 2) * 256:(q % 2 + 1) * 256],
                                          qh[:, q, k * P:(k + 1) * P], kmh[:, q % 2, :],
                                          start=True, stop=True)
                mm.then_inc(s_sn, 1)

            def negmax_transposed(b, j):
                pe.wait_ge(s_nm, at(b, NJ, j + 1))
                pe.wait_ge(s_ql, at(b, NJ, j + 1))
                pe.wait_ge(s_x1, at(b, NJ, j))
                for k in range(NT):
                    mm = nc.tensor.transpose(ps[0:32, 0, k * P:(k + 1) * P], nm[:, k, :].bitcast(F32), ident)
                mm.then_inc(s_nTp, 1)

            def scores_transposed(b, j, front):
                if front:
                    pe.wait_ge(s_mT, at(b, NJ, j + 2))
                pe.wait_ge(s_nrow, at(b, 16 * NJ * NQ, (j + 1) * NQ * 16))
                pe.wait_ge(s_mx, at(b, NJ * NT, (j + 1) * NT))
                for p in range(NPAIR):
                    q, c = p // 2, slice((p % 2) * P, (p % 2 + 1) * P)
                    bank = 2 + p % 4
                    if p >= 4 and p % 2 == 0:
                        pe.wait_ge(s_e, at(b, NJ * 4, j * 4 + p // 2 - 1))
                    nc.tensor.matmul(ps[:, bank, :], kmh[:, q % 2, c], qh[:, q, :], start=True, stop=False)
                    nc.tensor.matmul(ps[:, bank, :], kml[:, q % 2, c], qh[:, q, :], start=False, stop=False)
                    nc.tensor.matmul(ps[:, bank, :], kms[:, q, c], ql[:, q, :],
                                     start=False, stop=True).then_inc(s_st, 1)

            def pv(b, j, front):
                if front:
                    pe.wait_ge(s_ql, at(b, NJ, j + 2))
                else:
                    pe.wait_ge(s_x2T, at(b, NJ, j))
                for half in range(2):
                    pe.wait_ge(s_e, at(b, NJ * 4, j * 4 + 2 * half + 2))
                    for p in range(4):
                        mm = nc.tensor.matmul(ps[32 * p:32 * p + 32, half, :], vd[:, :], e[:, 4 * half + p, :],
                                              start=True, stop=True)
                mm.then_inc(s_o, 1)
                for p in range(NPAIR):
                    for k in range(NT):
                        mm = nc.tensor.matmul(ps[32 * k:32 * k + 32, 2, 0:P], cst[:, C_E + 32 * p:C_E + 32 * p + 32],
                                              e[:, p, k * P:(k + 1) * P], start=(p == 0), stop=(p == NPAIR - 1))
                mm.then_inc(s_dn, 1)

            def spread(b, j):
                pe.wait_ge(s_rd, at(b, NJ, j + 1))
                for c in range(KD):
                    for k in range(NT):
                        w = C_BC + (c * NT + k) * P
                        mm = nc.tensor.matmul(ps[:, 4 + c, k * P:(k + 1) * P], cst[:, w:w + P], rD[:, :],
                                              start=True, stop=True)
                mm.then_inc(s_bc, 1)

            def project_out(b, j):
                pe.wait_ge(s_osb, at(b, NJ, j + 1))
                pe.wait_ge(s_oT, at(b, NJ, j + 1))
                for k in range(NT):
                    for c in range(KD):
                        mm = nc.tensor.matmul(ps[:, k // 2, (k % 2) * D:(k % 2 + 1) * D], osb[:, c, k * P:(k + 1) * P],
                                              wo[:, c, :], start=(c == 0), stop=(c == KD - 1))
                mm.then_inc(s_wo, 1)

            def t2(b, j, front):
                if front:
                    pe.wait_ge(s_nT, at(b, NJ, j + 2))
                pe.wait_ge(s_ln2, at(b, NJ, j + 1))
                for c in range(KD):
                    for k in range(NT):
                        mm = nc.tensor.transpose(ps[:, c, k * P:(k + 1) * P], xh2[:, j, k, c * P:(c + 1) * P], ident)
                mm.then_inc(s_x2p, 1)

            def take_slot(b, j, u):
                n, bank = slot(j, u)
                before = n - 2
                by_act = BY_ACT[before % NU]
                if by_act:
                    pe.wait_ge(s_fa, at(b, NJ * NFA, reads_before(before + 1, True)))
                elif before < 0:
                    pe.wait_ge(s_fv, 1 + at(b, NJ * NFV, 0))
                else:
                    pe.wait_ge(s_fv, 1 + at(b, NJ * NFV, reads_before(before + 1, False)))
                return ps[:, bank, :]

            def w1(b, j, m):
                o = take_slot(b, j, f"h{m}")
                js, ms = slice(j * CH, (j + 1) * CH), slice(m * P, (m + 1) * P)
                three_pass(o, (lambda k: w1h[:, k, ms], lambda k: w1l[:, k, ms]),
                           (lambda k: xmh[:, k, js], lambda k: xml[:, k, js]), False).then_inc(s_f, 1)

            def gate(b, j):
                o = take_slot(b, j, "gate")
                pe.wait_ge(s_fa, at(b, NJ * NFA, j * NFA + 1))
                for k in range(NT):
                    mm = nc.tensor.matmul(o[:, k * NPATH:(k + 1) * NPATH], thT[DM:, k * P:(k + 1) * P],
                                          wo2[DM:, :], start=True, stop=True)
                mm.then_inc(s_f, 1)

            def rep(b, j, m):
                o = take_slot(b, j, f"rep{m}")
                if m == 0:
                    pe.wait_ge(s_oh, at(b, NJ, j + 1))
                for k in range(NT):
                    ks = slice(k * P, (k + 1) * P)
                    for a in range(2):
                        p = 2 * m + a
                        if p < NPATH:
                            sel = oh[:, k, p:p + 1].broadcast_to([P, DM])
                            mm = nc.tensor.matmul(o[a * DM:(a + 1) * DM, ks], sel, ident_b[:, :], start=True, stop=True)
                        else:
                            mm = nc.tensor.matmul(o[DM:DM + NPATH, ks], oh[:, k, 0:NPATH], ident_b[:, :],
                                                  start=True, stop=True)
                mm.then_inc(s_f, 1)

            def w2_product(b, j, i):
                o = take_slot(b, j, ("w2a", "w2b")[i])
                pe.wait_ge(s_hh, at(b, NJ * NM, (j + 1) * NM))
                pe.wait_ge(s_hl, 1 + at(b, NJ * NM, (j + 1) * NM))
                for k in (2 * i, 2 * i + 1):
                    ks, n = slice(k * P, (k + 1) * P), 0
                    for h, w in ((hmh, w2h), (hml, w2h), (hmh, w2l)):
                        for m in range(NM):
                            r = P if m < 4 else DM + NPATH
                            n += 1
                            mm = nc.tensor.matmul(o[:, (k % 2) * D:(k % 2 + 1) * D], h[0:r, m, ks], w[0:r, m, :],
                                                  start=(n == 1), stop=(n == 3 * NM))
                mm.then_inc(s_f, 1)

            def mixed(b, j):
                pe.wait_ge(s_xmh, at(b, NJ * KD, (j + 1) * KD))
                pe.wait_ge(s_xml, at(b, NJ * KD, (j + 1) * KD))

            def step(n, front, f):
                if front:
                    t1(*front)
                if n:
                    scores_transposed(*n, front)
                if front:
                    wq(*front)
                if f:
                    mixed(*f)
                    w1(*f, 4)
                    gate(*f)
                    w1(*f, 0)
                    w1(*f, 1)
                if n:
                    pv(*n, front)
                if f:
                    w1(*f, 2)
                    w1(*f, 3)
                if n:
                    spread(*n)
                if f:
                    rep(*f, 0)
                    rep(*f, 1)
                if front:
                    scores_for_max(*front, (0, 1))
                if n:
                    project_out(*n)
                if f:
                    rep(*f, 2)
                    rep(*f, 3)
                    rep(*f, 4)
                if front:
                    scores_for_max(*front, (2, 3))
                if f:
                    w2_product(*f, 0)
                if front:
                    negmax_transposed(*front)
                if f:
                    w2_product(*f, 1)
                if n:
                    t2(*n, front)

            pe.wait_ge(s_id, 1)
            pe.wait_ge(s_wqh, 1)
            pe.wait_ge(s_wql, 1)
            pe.wait_ge(s_setup_v, 5)
            step(None, (0, 0), None)
            step((0, 0), (0, 1), None)
            step((0, 1), (1, 0), None)
            for done in (s_w1h, s_w1l, s_w2h, s_w2l):
                pe.wait_ge(done, 1)
            with pe.Fori(1, B - 1) as r:
                step((r, 0), (r, 1), (r - 1, 0))
                step((r, 1), (r + 1, 0), (r - 1, 1))
            step((B - 1, 0), (B - 1, 1), (B - 2, 0))
            step((B - 1, 1), None, (B - 2, 1))
            step(None, None, (B - 1, 0))
            step(None, None, (B - 1, 1))

        @block.scalar
        def _(act):
            act.wait_ge(s_wa, 16 * WA_LOADS)
            nc.scalar.activation(wqh[:, :, :], wq32, ACT.Copy).then_inc(s_wqh, 1)

            def split_ffn_weights():
                act.wait_ge(s_wf, 16 * WF_LOADS)
                nc.scalar.activation(w1h[:, :, :], w1_32, ACT.Copy).then_inc(s_w1h, 1)
                nc.scalar.activation(w2h[:, 0:4, :], w2_32[:, 0:4, :], ACT.Copy)
                r = DM + NPATH
                nc.scalar.activation(w2h[0:r, 4, :], w2_32[0:r, 4, :], ACT.Copy).then_inc(s_w2h, 1)

            def copies_t1(b, j):
                act.wait_ge(s_mTp, at(b, NJ, j + 1))
                act.wait_ge(s_mrow, at(b, 16 * NJ * NQ, j * NQ * 16))
                nc.scalar.activation(mT[:, :], ps_b, ACT.Copy).then_inc(s_mT, 1)
                act.wait_ge(s_xTp, at(b, NJ, j + 1))
                act.wait_ge(s_qp, at(b, NJ * KD, j * KD))
                for c in range(KD):
                    nc.scalar.activation(xTh[:, c, :], ps[:, c, :], ACT.Copy).then_inc(s_xTh, 1)

            def q_hi(b, j):
                act.wait_ge(s_st, at(b, NJ * NPAIR, j * NPAIR))
                for m in range(KD):
                    act.wait_ge(s_qp, at(b, NJ * KD, j * KD + m + 1))
                    for par in range(2):
                        r, _ = halves(par)
                        a = nc.scalar.activation(qh[r, 2 * m + par, :], ps[r, m, :], ACT.Identity, bias=bqs[r, m:m + 1])
                a.then_inc(s_qh, 1)

            def maxima(b, j):
                act.wait_ge(s_nTp, at(b, NJ, j + 1))
                act.wait_ge(s_nrow, at(b, 16 * NJ * NQ, j * NQ * 16))
                nc.scalar.activation(nmT, ps[0:32, 0, :], ACT.Copy).then_inc(s_nT, 1)

            def softmax_exp(b, j):
                act.wait_ge(s_dn, at(b, NJ, j))
                for i in range(4):
                    act.wait_ge(s_st, at(b, NJ * NPAIR, j * NPAIR + 2 * i + 2))
                    bank = 2 + 2 * (i % 2)
                    nc.scalar.activation(e[:, 2 * i:2 * i + 2, :], ps[:, bank:bank + 2, :], ACT.Exp).then_inc(s_e, 1)

            def pv_copy(b, j):
                act.wait_ge(s_o, at(b, NJ, j + 1))
                act.wait_ge(s_wo, at(b, NJ, j))
                nc.scalar.activation(osb[:, :, :], ps[:, 0:2, :], ACT.Copy).then_inc(s_osb, 1)

            def copy_t2(b, j):
                act.wait_ge(s_x2p, at(b, NJ, j + 1))
                act.wait_ge(s_xm, at(b, NJ * KD, 0))
                nc.scalar.activation(x2T[:, :, 1 + j * CH:1 + (j + 1) * CH], ps[:, 0:2, :], ACT.Copy).then_inc(s_x2T, 1)

            def mixed_hi(b, j):
                for c in range(KD):
                    act.wait_ge(s_xm, at(b, NJ * KD, j * KD + c + 1))
                    nc.scalar.activation(xmh[:, c, j * CH:(j + 1) * CH], xm[:, c, :], ACT.Copy).then_inc(s_xmh, 1)

            def hidden(b, j, m):
                n, bank = slot(j, f"h{m}")
                act.wait_ge(s_f, at(b, NJ * NU, n + 1))
                if m == 4:
                    act.wait_ge(s_hl, 1 + at(b, NJ * NM, j * NM))
                    nc.scalar.activation(thT[DM:, :], ps[DM:, bank, :], ACT.Tanh, bias=b1s[DM:, 4:5])
                    nc.scalar.activation(hs[0:DM, 4, :], ps[0:DM, bank, :], ACT.Identity,
                                         bias=b1s[0:DM, 4:5]).then_inc(s_fa, 1)
                else:
                    nc.scalar.activation(hs[:, m, :], ps[:, bank, :], ACT.Identity, bias=b1s[:, m:m + 1]).then_inc(s_fa, 1)

            def keep_xh2(b, j):
                act.wait_ge(s_yg, 1 + at(b, NJ, j))
                nc.scalar.activation(xh2f[:, :, :], xh2[:, j], ACT.Copy).then_inc(s_xh2f, 1)

            def selected_hi(b, j, m):
                act.wait_ge(s_fv, 1 + at(b, NJ * NFV, j * NFV + m + 2))
                if m < 4:
                    nc.scalar.activation(hmh[:, m, :], hs[:, m, :], ACT.Copy).then_inc(s_hh, 1)
                else:
                    r = DM + NPATH
                    nc.scalar.activation(hmh[0:r, 4, :], h4s[0:r, :], ACT.Copy).then_inc(s_hh, 1)

            def step(n, front, f):
                if front:
                    copies_t1(*front)
                if n:
                    softmax_exp(*n)
                if f and f[1] == 0:
                    mixed_hi(*f)
                if front:
                    q_hi(*front)
                if f:
                    hidden(*f, 4)
                    hidden(*f, 0)
                    hidden(*f, 1)
                if f and f[1] == 0:
                    mixed_hi(f[0], 1)
                if n:
                    pv_copy(*n)
                if f:
                    hidden(*f, 2)
                    hidden(*f, 3)
                    keep_xh2(*f)
                    for m in range(NM):
                        selected_hi(*f, m)
                if front:
                    maxima(*front)
                if n:
                    copy_t2(*n)

            step(None, (0, 0), None)
            step((0, 0), (0, 1), None)
            split_ffn_weights()
            step((0, 1), (1, 0), None)
            act.wait_ge(s_w1l, 1)
            act.wait_ge(s_w2l, 1)
            act.wait_ge(s_ones, 1)
            with act.Fori(1, B - 1) as r:
                step((r, 0), (r, 1), (r - 1, 0))
                step((r, 1), (r + 1, 0), (r - 1, 1))
            step((B - 1, 0), (B - 1, 1), (B - 2, 0))
            step((B - 1, 1), None, (B - 2, 1))
            step(None, None, (B - 1, 0))
            step(None, None, (B - 1, 1))

        @block.vector
        def _(dve):
            v = nc.vector
            dve.wait_ge(s_cst, 16)
            v.tensor_copy(ident_b[:, :], ident).then_inc(s_id, 1)
            v.memset(kml[:, :, :].bitcast(F32), 0.0).then_inc(s_fv, 1)
            v.memset(ql[:, :, :].bitcast(F32), 0.0)
            v.memset(x2T[:, :, 0:1], 0.0)
            v.memset(x2T[:, :, S + 1:S + 2], 0.0)
            v.memset(oh[:, :, :], 0.0)
            for q in range(NQ):
                _, m = halves(q % 2)
                v.tensor_copy(kms[m, q, :], cst[m, C_SEL + q * 256:C_SEL + (q + 1) * 256])
            for par in range(2):
                _, m = halves(par)
                a = v.tensor_copy(kmh[m, par, :], cst[m, C_IDK:C_IDK + 256])
            a.then_inc(s_init, 1)

            dve.wait_ge(s_wa, 16 * WA_LOADS)
            v.tensor_copy(wk8[:, :, :].rearrange("p c (h d) -> p c h d", h=8),
                          wk[:, :, :].rearrange("p c (h d) -> p c h d", h=1).broadcast_to([P, KD, 8, DK])).then_inc(s_setup_v, 1)
            dve.wait_ge(s_setup_pe, 1)
            for a in range(2):
                ins = v.tensor_copy(ctxT[:, :, :, a, :], ps[:, 0, :].rearrange("p (c b s) -> p c b s", c=KD, b=B))
            ins.then_inc(s_setup_v, 1)
            dve.wait_ge(s_setup_pe, 2)
            v.tensor_scalar(krep[:, :, :], ps[:, 1, 0:B * SK].rearrange("p (b s) -> p b s", b=B), bks[:, 0:1],
                            float(DK) ** -0.5, ALU.add, ALU.mult).then_inc(s_setup_v, 1)
            dve.wait_ge(s_setup_v, 3)
            v.tensor_copy(khi[:, :, :], krep[:, :, :]).then_inc(s_setup_v, 1)
            dve.wait_ge(s_setup_pe, 3)
            dve.wait_ge(s_setup_v, 4)
            v.tensor_tensor(klo[:, :, :], krep[:, :, :], khi[:, :, :].bitcast(F32), ALU.subtract)
            v.tensor_tensor(vall[:, :, :], ps[:, 2, 0:B * DK].rearrange("p (b d) -> p b d", b=B),
                            bvs[:, :].rearrange("p (b d) -> p b d", b=1).broadcast_to([P, B, DK]),
                            ALU.add).then_inc(s_setup_v, 1)

            def wq_lo():
                dve.wait_ge(s_wqh, 1)
                v.tensor_tensor(wql[:, :, :], wq32, wqh[:, :, :].bitcast(F32), ALU.subtract).then_inc(s_wql, 1)

            def ffn_weights_lo():
                dve.wait_ge(s_w1h, 1)
                v.tensor_tensor(w1l[:, :, :], w1_32, w1h[:, :, :].bitcast(F32), ALU.subtract).then_inc(s_w1l, 1)
                dve.wait_ge(s_w2h, 1)
                v.tensor_tensor(w2l[:, 0:4, :], w2_32[:, 0:4, :], w2h[:, 0:4, :].bitcast(F32), ALU.subtract)
                r = DM + NPATH
                v.tensor_tensor(w2l[0:r, 4, :], w2_32[0:r, 4, :], w2h[0:r, 4, :].bitcast(F32),
                                ALU.subtract).then_inc(s_w2l, 1)
                dve.wait_ge(s_w2l, 1)
                v.memset(hs[DM:, 4, :], 1.0).then_inc(s_ones, 1)

            def stats(src, ln, sems, count):
                st, su, dm, mu, va, vb, ve, _ = ln
                s_stats, s_halves, s_parts, s_var = sems
                for k in range(NT):
                    a = v.bn_stats(st[:, k].rearrange("p a c -> p (a c)"), src(k))
                a.then_inc(s_stats, 1)
                dve.wait_ge(s_stats, count)
                v.tensor_tensor(su[:, :, :], st[:, :, 0, :], st[:, :, 1, :], ALU.add)
                v.tensor_tensor(dm[:, :], st[:, :, 0, 1], st[:, :, 1, 1], ALU.subtract).then_inc(s_halves, 1)
                dve.wait_ge(s_halves, count)
                v.tensor_scalar(mu[:, :], su[:, :, 1], 0.5, None, ALU.mult)
                v.tensor_scalar(va[:, :], su[:, :, 2], 1.0 / D, EPS, ALU.mult, ALU.add)
                v.scalar_tensor_tensor(out=vb[:, :], in0=dm[:, :], scalar=0.25, in1=dm[:, :],
                                       op0=ALU.mult, op1=ALU.mult).then_inc(s_parts, 1)
                dve.wait_ge(s_parts, count)
                v.tensor_tensor(ve[:, :], va[:, :], vb[:, :], ALU.add).then_inc(s_var, 1)

            def normalise(dst, src, ln, s_r, s_done, count):
                dve.wait_ge(s_r, count)
                for k in range(NT):
                    a = v.tensor_scalar(dst(k), src(k), ln[3][:, k:k + 1], ln[7][:, k:k + 1], ALU.subtract, ALU.mult)
                a.then_inc(s_done, 1)

            def layernorm1_stats(b, j):
                c = at(b, NJ, j + 1)
                dve.wait_ge(s_x[j], at(b, 16, 16))
                stats(lambda k: xin[:, j, k, :], ln1, (s_ln1s, s_ln1h, s_ln1p, s_ln1v), c)
                dve.wait_ge(s_m[j], at(b, 16, 16))
                dve.wait_ge(s_mTp, at(b, NJ, j))
                v.tensor_scalar(mb[:, :, :, :], min_[:, j].rearrange("p k (a s) -> p k a s", a=1).broadcast_to([P, NT, 2, SK]),
                                0, MASKED, ALU.is_equal, ALU.mult).then_inc(s_mb, 1)

            def layernorm1_apply(b, j):
                c = at(b, NJ, j + 1)
                dve.wait_ge(s_xTp, at(b, NJ, j))
                normalise(lambda k: xh1[:, k, :], lambda k: xin[:, j, k, :], ln1, s_ln1r, s_ln1, c)

            def x_lo(b, j):
                dve.wait_ge(s_qp, at(b, NJ * KD, j * KD))
                for c in range(KD):
                    dve.wait_ge(s_xTh, at(b, NJ * KD, j * KD + c + 1))
                    a = v.tensor_tensor(xTl[:, c, :], ps[:, c, :], xTh[:, c, :].bitcast(F32), ALU.subtract)
                a.then_inc(s_xTl, 1)

            def q_lo(b, j):
                dve.wait_ge(s_qh, at(b, NJ, j + 1))
                for m in range(KD):
                    for par in range(2):
                        r, _ = halves(par)
                        a = v.scalar_tensor_tensor(out=ql[r, 2 * m + par, :], in0=ps[r, m, :], scalar=bqs[r, m:m + 1],
                                                   in1=qh[r, 2 * m + par, :].bitcast(F32), op0=ALU.add, op1=ALU.subtract)
                a.then_inc(s_ql, 1)

            def take_max(b, j, tiles):
                for k in tiles:
                    dve.wait_ge(s_sn, at(b, NJ * NT, j * NT + k + 1))
                    bank = 2 + 2 * (k % 2)
                    v.tensor_reduce(mx[:, k, :].rearrange("p (a h) -> p a h", a=2),
                                    ps[:, bank:bank + 2, :].rearrange("p a (h s) -> p a h s", s=SK),
                                    AX.X, ALU.max).then_inc(s_mx, 1)

            def negate_max(b, j):
                dve.wait_ge(s_mx, at(b, NJ * NT, (j + 1) * NT))
                v.tensor_scalar(nm[:, :, 0:H], mx[:, :, :], -1.0, None, ALU.mult).then_inc(s_nmh, 1)
                dve.wait_ge(s_nmh, at(b, NJ, j + 1))
                v.scalar_tensor_tensor(out=nm[:, :, H:2 * H], in0=mx[:, :, :], scalar=-1.0,
                                       in1=nm[:, :, 0:H].bitcast(F32), op0=ALU.mult, op1=ALU.subtract).then_inc(s_nm, 1)

            def invert(b, j):
                dve.wait_ge(s_dn, at(b, NJ, j + 1))
                v.reciprocal(rD[:, :], ps[:, 2, 0:P]).then_inc(s_rd, 1)

            def attn_normalise(b, j):
                dve.wait_ge(s_bc, at(b, NJ, j + 1))
                dve.wait_ge(s_osb, at(b, NJ, j + 1))
                v.tensor_tensor(osb[:, :, :], osb[:, :, :], ps[:, 4:6, :], ALU.mult).then_inc(s_oT, 1)

            def x1_stats(b, j):
                c = at(b, NJ, j + 1)
                dve.wait_ge(s_xb, c)
                dve.wait_ge(s_wo, c)
                xj = x1[:, j].rearrange("p (a k) d -> p a (k d)", a=2)
                v.tensor_tensor(xj, ps[:, 0:2, :], xj, ALU.add).then_inc(s_x1, 1)
                dve.wait_ge(s_x1, c)
                stats(lambda k: x1[:, j, k, :], ln2, (s_ln2s, s_ln2h, s_ln2p, s_ln2v), c)

            def layernorm2_apply(b, j, f):
                c = at(b, NJ, j + 1)
                if f:
                    dve.wait_ge(s_xh2f, at(f[0], NJ, f[1] + 1))
                normalise(lambda k: xh2[:, j, k, :], lambda k: x1[:, j, k, :], ln2, s_ln2r, s_ln2, c)

            def mix(b, j):
                dve.wait_ge(s_x2T, at(b, NJ, NJ))
                for c in range(KD):
                    n = at(b, NJ * KD, j * KD + c + 1)
                    t = j * CH
                    if j > 0:
                        dve.wait_ge(s_xml, at(b, NJ * KD, (j - 1) * KD + c + 1))
                        dve.wait_ge(s_xmh, at(b, NJ * KD, (j - 1) * KD + c + 1))
                    v.tensor_scalar(xm[:, c, :], x2T[:, c, t:t + CH], mks[:, 0, c:c + 1], None, ALU.mult).then_inc(s_mix1, 1)
                    dve.wait_ge(s_mix1, n)
                    v.scalar_tensor_tensor(out=xm[:, c, :], in0=x2T[:, c, t + 1:t + 1 + CH], scalar=mks[:, 1, c:c + 1],
                                           in1=xm[:, c, :], op0=ALU.mult, op1=ALU.add).then_inc(s_mix2, 1)
                    dve.wait_ge(s_mix2, n)
                    v.scalar_tensor_tensor(out=xm[:, c, :], in0=x2T[:, c, t + 2:t + 2 + CH], scalar=mks[:, 2, c:c + 1],
                                           in1=xm[:, c, :], op0=ALU.mult, op1=ALU.add).then_inc(s_xm, 1)

            def argmax(b, j):
                n, bank = slot(j, "gate")
                c = at(b, NJ, j + 1)
                dve.wait_ge(s_f, at(b, NJ * NU, n + 1))
                v.tensor_tensor(gs[:, :, :], ps[:, bank, 0:NT * NPATH].rearrange("p (k n) -> p k n", n=NPATH),
                                bo2s[:, :].rearrange("p (k n) -> p k n", k=1).broadcast_to([P, NT, NPATH]),
                                ALU.add).then_inc(s_fv, 1)
                dve.wait_ge(s_fv, 1 + at(b, NJ * NFV, j * NFV + 1))
                v.tensor_reduce(gmax[:, :], gs[:, :, :], AX.X, ALU.max).then_inc(s_g2, 1)
                dve.wait_ge(s_g2, c)
                iota = cst[:, C_IO:C_IO + NPATH].rearrange("p (k n) -> p k n", k=1).broadcast_to([P, NT, NPATH])

                def per_tile(t):
                    return t[:, :].rearrange("p (k n) -> p k n", n=1).broadcast_to([P, NT, NPATH])

                v.tensor_tensor(cand[:, :, :], gs[:, :, :], per_tile(gmax), ALU.is_ge).then_inc(s_g3, 1)
                dve.wait_ge(s_g3, at(b, 2 * NJ, 2 * j + 1))
                v.tensor_tensor(gs[:, :, :], cand[:, :, :], iota, ALU.mult).then_inc(s_g3, 1)
                dve.wait_ge(s_g3, at(b, 2 * NJ, 2 * j + 2))
                v.tensor_reduce(gidx[:, :], gs[:, :, :], AX.X, ALU.min).then_inc(s_g4, 1)
                dve.wait_ge(s_g4, c)
                v.tensor_tensor(oh[:, :, 0:NPATH], iota, per_tile(gidx), ALU.is_equal).then_inc(s_oh, 1)

            def select(b, j, m):
                n, bank = slot(j, f"rep{m}")
                if m == 0:
                    dve.wait_ge(s_fa, at(b, NJ * NFA, (j + 1) * NFA))
                dve.wait_ge(s_f, at(b, NJ * NU, n + 1))
                r = P if m < 4 else DM + NPATH
                dst = hs[:, m, :] if m < 4 else h4s[0:r, :]
                v.tensor_tensor(dst, hs[0:r, m, :], ps[0:r, bank, :], ALU.mult).then_inc(s_fv, 1)

            def residual_stats(b, j):
                c = at(b, NJ, j + 1)
                dve.wait_ge(s_xh2f, c)
                for i, u in enumerate(("w2a", "w2b")):
                    n, bank = slot(j, u)
                    dve.wait_ge(s_f, at(b, NJ * NU, n + 1))
                    v.tensor_tensor(xh2f[:, 2 * i:2 * i + 2, :], xh2f[:, 2 * i:2 * i + 2, :],
                                    ps[:, bank, :].rearrange("p (k d) -> p k d", d=D), ALU.add).then_inc(s_fv, 1)
                dve.wait_ge(s_fv, 1 + at(b, NJ * NFV, (j + 1) * NFV))
                stats(lambda k: xh2f[:, k, :], ln3, (s_ln3s, s_ln3h, s_ln3p, s_ln3v), c)

            def layernorm3_apply(b, j):
                c = at(b, NJ, j + 1)
                normalise(lambda k: xh2f[:, k, :], lambda k: xh2f[:, k, :], ln3, s_ln3r, s_ln3, c)

            def step(n, front, f, after):
                if front:
                    x_lo(*front)
                if f and f[1] == 0:
                    mix(*f)
                if front:
                    q_lo(*front)
                if f:
                    argmax(*f)
                if f and f[1] == 0:
                    mix(f[0], 1)
                if n:
                    invert(*n)
                    attn_normalise(*n)
                if f:
                    select(*f, 0)
                    select(*f, 1)
                if front:
                    take_max(*front, (0, 1))
                if f:
                    select(*f, 2)
                    select(*f, 3)
                    select(*f, 4)
                if front:
                    take_max(*front, (2, 3))
                    negate_max(*front)
                if n:
                    x1_stats(*n)
                if after:
                    layernorm1_stats(*after)
                if n:
                    layernorm2_apply(*n, f)
                if after:
                    layernorm1_apply(*after)
                if f:
                    residual_stats(*f)
                    layernorm3_apply(*f)

            layernorm1_stats(0, 0)
            layernorm1_apply(0, 0)
            wq_lo()
            step(None, (0, 0), None, (0, 1))
            step((0, 0), (0, 1), None, (1, 0))
            ffn_weights_lo()
            step((0, 1), (1, 0), None, (1, 1))
            with dve.Fori(1, B - 1) as r:
                step((r, 0), (r, 1), (r - 1, 0), (r + 1, 0))
                step((r, 1), (r + 1, 0), (r - 1, 1), (r + 1, 1))
            step((B - 1, 0), (B - 1, 1), (B - 2, 0), None)
            step((B - 1, 1), None, (B - 2, 1), None)
            step(None, None, (B - 1, 0), None)
            step(None, None, (B - 1, 1), None)

        @block.gpsimd
        def _(pool):
            g = nc.gpsimd
            g.memset(halfneg[:, :], -0.5).then_inc(s_init, 1)
            g.memset(unused[:, 0:1], 0.0).then_inc(s_yg, 1)
            g.memset(unused[:, 1:2], 0.0).then_inc(s_yo, 1)
            g.memset(unused[:, 2:3], 0.0).then_inc(s_out[1], 16)
            g.memset(unused[:, 3:4], 0.0).then_inc(s_hl, 1)
            pool.wait_ge(s_init, 2)
            pool.wait_ge(s_setup_v, 5)

            def operands(b):
                pool.wait_ge(s_st, at(b, NJ * NPAIR, 0))

                def keys(src, rows):
                    k = src[rows, bass.ds(b, 1), :]
                    return k.broadcast_to([64, 4, SK])

                def d4(rows):
                    return cst[rows, C_D4:C_D4 + 256].rearrange("p (h s) -> p h s", h=4)

                def to(dst, rows, i):
                    return dst[rows, i, :].rearrange("p (h s) -> p h s", h=4)

                for par in range(2):
                    r, _ = halves(par)
                    g.tensor_tensor(to(kmh, r, par), keys(khi[:, :, :].bitcast(F32), r), d4(r), ALU.mult)
                    g.tensor_tensor(to(kml, r, par), keys(klo, r), d4(r), ALU.mult)
                    for q in (par, par + 2):
                        a = g.tensor_tensor(to(kms, r, q), keys(khi[:, :, :].bitcast(F32), r), d4(r), ALU.mult)
                    a.then_inc(s_km, 1)
                    pool.wait_ge(s_km, at(b, 3, par + 1))
                pool.wait_ge(s_dn, at(b, NJ, 0))
                g.tensor_tensor(vd[:, :].rearrange("p (h d) -> p h d", h=2), vall[:, bass.ds(b, 1), :].broadcast_to([P, 2, DK]),
                                cst[:, C_VM:C_VM + 32].rearrange("p (h d) -> p h d", h=2), ALU.mult).then_inc(s_km, 1)

            def rstd(ln, s_v, s_r, c):
                pool.wait_ge(s_v, c)
                g.tensor_tensor(ln[7][:, :], ln[6][:, :], halfneg[:, :], ALU.pow).then_inc(s_r, 1)

            def add_bo(b, j, f):
                if f:
                    pool.wait_ge(s_x1b, at(f[0], NJ, f[1] + 1))
                pool.wait_ge(s_x[j], at(b, 16, 16))
                g.tensor_tensor(x1[:, j], xin[:, j], bos[:, :].rearrange("p (k d) -> p k d", k=1).broadcast_to([P, NT, D]),
                                ALU.add).then_inc(s_xb, 1)

            def add_beta(b, j):
                pool.wait_ge(s_yo, 1 + at(b, NJ, j))
                g.tensor_tensor(x1b[:, :, :], x1[:, j], bts[:, :].rearrange("p (k d) -> p k d", k=1).broadcast_to([P, NT, D]),
                                ALU.add).then_inc(s_x1b, 1)

            def mixed_lo(b, j):
                for c in range(KD):
                    pool.wait_ge(s_xmh, at(b, NJ * KD, j * KD + c + 1))
                    js = slice(j * CH, (j + 1) * CH)
                    g.tensor_tensor(xml[:, c, js], xm[:, c, :], xmh[:, c, js].bitcast(F32), ALU.subtract).then_inc(s_xml, 1)

            def finish(b, j):
                c = at(b, NJ, j + 1)
                pool.wait_ge(s_ln3, c)
                if j == 0:
                    pool.wait_ge(s_out[1], at(b, 16, 16))
                else:
                    pool.wait_ge(s_out[0], at(b, 16, 16))
                g.tensor_tensor(y[:, :, :], xh2f[:, :, :], gms[:, :].rearrange("p (k d) -> p k d", k=1).broadcast_to([P, NT, D]),
                                ALU.mult).then_inc(s_yg, 1)
                pool.wait_ge(s_yg, 1 + c)
                pool.wait_ge(s_x1b, c)
                g.tensor_tensor(y[:, :, :], y[:, :, :], x1b[:, :, :], ALU.add).then_inc(s_yo, 1)

            def selected_lo(b, j, m):
                pool.wait_ge(s_hh, at(b, NJ * NM, j * NM + m + 1))
                r = P if m < 4 else DM + NPATH
                src = hs[:, m, :] if m < 4 else h4s[0:r, :]
                g.tensor_tensor(hml[0:r, m, :], src, hmh[0:r, m, :].bitcast(F32), ALU.subtract).then_inc(s_hl, 1)

            def step(n, front, f, after):
                if f and f[1] == 0:
                    mixed_lo(*f)
                if f:
                    add_beta(*f)
                if n:
                    add_bo(*n, f)
                if f and f[1] == 0:
                    mixed_lo(f[0], 1)
                if front and front[1] == 0:
                    operands(front[0])
                if f:
                    for m in range(NM):
                        selected_lo(*f, m)
                if n:
                    rstd(ln2, s_ln2v, s_ln2r, at(n[0], NJ, n[1] + 1))
                if after:
                    rstd(ln1, s_ln1v, s_ln1r, at(after[0], NJ, after[1] + 1))
                if f:
                    rstd(ln3, s_ln3v, s_ln3r, at(f[0], NJ, f[1] + 1))
                if f:
                    finish(*f)

            pool.wait_ge(s_wa, 16 * WA_LOADS)
            rstd(ln1, s_ln1v, s_ln1r, 1)
            step(None, (0, 0), None, (0, 1))
            step((0, 0), (0, 1), None, (1, 0))
            pool.wait_ge(s_wf, 16 * WF_LOADS)
            step((0, 1), (1, 0), None, (1, 1))
            with pool.Fori(1, B - 1) as r:
                step((r, 0), (r, 1), (r - 1, 0), (r + 1, 0))
                step((r, 1), (r + 1, 0), (r - 1, 1), (r + 1, 1))
            step((B - 1, 0), (B - 1, 1), (B - 2, 0), None)
            step((B - 1, 1), None, (B - 2, 1), None)
            step(None, None, (B - 1, 0), None)
            step(None, None, (B - 1, 1), None)


WA_LOADS = 5 + P // DK + 3
WF_LOADS = NPATH + 1 + 4 + 3 + 4

_PREFIX = ("L0_xattn_", "L0_ffn_")
_ATTN = ["Wq", "bq", "Wk", "bk", "Wv", "bv", "Wo", "bo"]
_FFN = ["mix_kernel", "W1", "b1", "W2", "b2", "Wo1", "bo1", "Wo2", "bo2", "gamma", "beta"]


def kernel(**inputs):
    from concourse import bacc
    from concourse.bass_utils import run_bass_kernel_spmd

    nc = bacc.Bacc("TRN2", target_bir_lowering=False, num_devices=1)
    names = ["x", "ctx_1024", "mask_Bx1xSxS2_ik1"] + [_PREFIX[0] + n for n in _ATTN] + [_PREFIX[1] + n for n in _FFN]
    arrays = {n: np.ascontiguousarray(inputs[n]) for n in names}
    arrays["constants"] = constants()
    args = [nc.dram_tensor(f"in_{n}", a.shape, mybir.dt.from_np(a.dtype), kind="ExternalInput").ap()
            for n, a in arrays.items()]
    out = nc.dram_tensor("out_0", (B, S, D), F32, kind="ExternalOutput").ap()
    layer_program(nc, *args, out)
    r = run_bass_kernel_spmd(nc, [{f"in_{n}": a for n, a in arrays.items()}], core_ids=[0])
    return r.results[0]["out_0"]
```

```python
from contextlib import ExitStack

import numpy as np

import concourse.bass as bass
from concourse import mybir

F32 = mybir.dt.float32
F32R = mybir.dt.float32r
BF16 = mybir.dt.bfloat16
I32 = mybir.dt.int32
ALU = mybir.AluOpType
ACT = mybir.ActivationFunctionType
AX = mybir.AxisListType

P = 128
B, S, D = 4, 1024, 256
SK = 64
H, DK = 16, 16
NPATH, DM = 9, 64
CH = 512
NJ = S // CH
NT = CH // P
KD = D // P
NQ = 4
NPAIR = H // 2
NM = 5
EPS = 1e-5
MASKED = -float(2.0 ** 100)

C_ID = 0
C_D4 = C_ID + P
C_IDK = C_D4 + 4 * SK
C_SEL = C_IDK + 4 * SK
C_E = C_SEL + NQ * 4 * SK
C_BC = C_E + NPAIR * 32
C_VM = C_BC + KD * NT * P
C_IO = C_VM + 32
C_N = C_IO + NPATH


def constants():
    c = np.zeros((P, C_N), np.float32)
    r = np.arange(P)[:, None]
    hk = np.arange(4 * SK)[None, :]
    c[:, C_ID:C_ID + P] = np.eye(P)
    c[:, C_D4:C_D4 + 4 * SK] = (r % 64) // DK == hk // SK
    c[:, C_IDK:C_IDK + 4 * SK] = r % 64 == hk % SK
    for q in range(NQ):
        c[:, C_SEL + q * 4 * SK:C_SEL + (q + 1) * 4 * SK] = (r % 64 < 32) & (r % 16 == 4 * q + hk // SK)
    for p in range(NPAIR):
        c[:, C_E + 32 * p:C_E + 32 * p + 32] = np.arange(32)[None, :] % 16 == 2 * p + r // 64
    for m in range(KD):
        for k in range(NT):
            at = C_BC + P * (m * NT + k)
            c[:, at:at + P] = r == 32 * k + 8 * m + np.arange(P)[None, :] // DK
    c[:, C_VM:C_VM + 32] = r // 64 == np.arange(32)[None, :] // DK
    c[:, C_IO:C_IO + NPATH] = np.arange(NPATH) - NPATH
    return c


def layer_program(nc, x, ctx, mask, Wq, bq, Wk, bk, Wv, bv, Wo, bo, mixk, W1, b1, W2, b2,
                  Wo1, bo1, Wo2, bo2, gamma, beta, consts, out):
    with ExitStack() as stack:
        def sb(name, shape, dt=F32):
            return stack.enter_context(nc.sbuf_tensor(name, shape, dt))

        def sem(name):
            return stack.enter_context(nc.semaphore(name))

        stack.enter_context(nc.allow_non_contiguous_dma("biases, one value per partition"))

        cst = sb("cst", [P, C_N])
        ident_b = sb("ident_b", [P, P], BF16)
        wqh, wql = sb("wqh", [P, KD, D], F32R), sb("wql", [P, KD, D], F32R)
        w1h, w1l = sb("w1h", [P, KD, NM * P], F32R), sb("w1l", [P, KD, NM * P], F32R)
        w2h, w2l = sb("w2h", [P, NM, D], F32R), sb("w2l", [P, NM, D], F32R)
        wo = sb("wo", [P, KD, D])
        wo2 = sb("wo2", [P, NPATH])
        wk = sb("wk", [P, KD, DK])
        wk8 = sb("wk8", [P, KD, P])
        wv = sb("wv", [P, KD, DK])
        bqs = sb("bqs", [P, KD])
        bks = sb("bks", [P, 1])
        bvs = sb("bvs", [P, DK])
        bos, gms, bts = sb("bos", [P, D]), sb("gms", [P, D]), sb("bts", [P, D])
        b1s = sb("b1s", [P, NM])
        bo2s = sb("bo2s", [P, NPATH])
        mks = sb("mks", [P, 3, KD])
        tables = sb("tables", [P, 4])
        spare = sb("spare", [P, 4])
        halfneg = sb("halfneg", [P, NT])
        khi = sb("khi", [P, B, SK], F32R)
        klo = sb("klo", [P, B, SK])
        krep = sb("krep", [P, B, SK])
        vall = sb("vall", [P, B, DK])
        kmh = sb("kmh", [P, 2, 4 * SK], F32R)
        kml = sb("kml", [P, 2, 4 * SK], F32R)
        kms = sb("kms", [P, NQ, 4 * SK], F32R)
        vd = sb("vd", [P, 2 * DK])
        def ln_buffers(n):
            return (sb(f"st{n}", [P, NT, 2, 3]), sb(f"su{n}", [P, NT, 3]), sb(f"dm{n}", [P, NT]), sb(f"mu{n}", [P, NT]),
                    sb(f"va{n}", [P, NT]), sb(f"vb{n}", [P, NT]), sb(f"ve{n}", [P, NT]), sb(f"rs{n}", [P, NT]))

        xin = sb("xin", [P, NJ, NT, D])
        min_ = sb("min_", [P, NJ, NT, SK], I32)
        mb = sb("mb", [P, NT, 2, SK], BF16)
        mT = sb("mT", [P, CH])
        ln1 = ln_buffers("1")
        ln2 = ln_buffers("2")
        ln3 = ln_buffers("3")
        xh1 = sb("xh1", [P, NT, D])
        xTh, xTl = sb("xTh", [P, KD, CH], F32R), sb("xTl", [P, KD, CH], F32R)
        qh = sb("qh", [P, NQ, CH], F32R)
        ql = sb("ql", [P, NQ, CH], F32R)
        mx = sb("mx", [P, NT, H])
        nm = sb("nm", [P, NT, 2 * H], F32R)
        e = sb("e", [P, NPAIR, CH])
        ctx_in = e[0:SK, 0:2, :].rearrange("p a (b d) -> p (a b) d", d=D)
        ctxT = e[:, 2:4, :].rearrange("p c (b a s) -> p c b a s", b=B, a=2)
        rD = sb("rD", [P, P])
        osb = sb("osb", [P, KD, CH])
        x1 = sb("x1", [P, NJ, NT, D])
        xh2 = sb("xh2", [P, NJ, NT, D])
        x2T = sb("x2T", [P, KD, S + 2])
        xm = sb("xm", [P, KD, CH])
        xmh, xml = sb("xmh", [P, KD, S], F32R), sb("xml", [P, KD, S], F32R)
        hs = sb("hs", [P, NM, CH])
        h4s = sb("h4s", [P, CH])
        hmh, hml = sb("hmh", [P, NM, CH], F32R), sb("hml", [P, NM, CH], F32R)
        wq32 = h4s[:, :].rearrange("p (c n) -> p c n", c=KD)
        hs_flat = hs[:, :, :].rearrange("p m t -> p (m t)")
        w1_32 = hs_flat[:, 0:KD * NM * P].rearrange("p (c n) -> p c n", c=KD)
        w2_32 = hs_flat[:, KD * NM * P:KD * NM * P + NM * D].rearrange("p (m n) -> p m n", m=NM)
        thT = sb("thT", [P, CH])
        nmT = thT[0:32, :]
        gs = sb("gs", [P, NT, NPATH])
        gmax = sb("gmax", [P, NT])
        cand = sb("cand", [P, NT, NPATH])
        gidx = sb("gidx", [P, NT])
        oh = sb("oh", [P, NT, NPATH + 1], BF16)
        x1b = sb("x1b", [P, NT, D])
        xh2f = sb("xh2f", [P, NT, D])
        y = sb("y", [P, NT, D])

        ps = stack.enter_context(nc.psum_tensor("ps", [P, 8, CH], F32))

        ident = cst[:, C_ID:C_ID + P]
        ps_b = ps[:, 2, 0:CH // 2].bitcast(BF16)

        s_ident, s_rows, s_cst = sem("identity_loaded"), sem("score_constants_loaded"), sem("other_constants_loaded")
        s_ctx, s_wk, s_wq = sem("context_loaded"), sem("key_value_weights_loaded"), sem("wq_loaded")
        s_wo_in, s_wf = sem("wo_loaded"), sem("ffn_weights_loaded")
        s_x = [sem(f"x_loaded{j}") for j in range(NJ)]
        s_m = [sem(f"mask_loaded{j}") for j in range(NJ)]
        s_init, s_kc = sem("memsets_done"), sem("constant_rows_placed")
        s_wqh, s_wql, s_w1h, s_w1l = sem("wq_hi"), sem("wq_lo"), sem("w1_hi"), sem("w1_lo")
        s_w2h, s_w2l, s_ones = sem("w2_hi"), sem("w2_lo"), sem("b2_selector_ones")
        s_id = sem("identity_in_bf16")
        s_setup_pe, s_setup_v = sem("setup_products"), sem("setup_copies")
        s_km = sem("score_operands_built")
        s_ln1s, s_ln1h, s_ln1p = sem("ln1_stats"), sem("ln1_halves"), sem("ln1_var_parts")
        s_ln1v, s_ln1r, s_ln1b, s_ln1 = sem("ln1_var"), sem("ln1_rstd"), sem("ln1_bias"), sem("ln1_done")
        s_ln2s, s_ln2h, s_ln2p = sem("ln2_stats"), sem("ln2_halves"), sem("ln2_var_parts")
        s_ln2v, s_ln2r, s_ln2 = sem("ln2_var"), sem("ln2_rstd"), sem("ln2_done")
        s_ln3s, s_ln3h, s_ln3p = sem("ln3_stats"), sem("ln3_halves"), sem("ln3_var_parts")
        s_ln3v, s_ln3r, s_ln3 = sem("ln3_var"), sem("ln3_rstd"), sem("ln3_done")
        s_mb, s_xb = sem("mask_bias"), sem("x_plus_bo")
        s_mTp, s_mT = sem("maskT_in_psum"), sem("maskT_copied")
        s_mrow = sem("mask_rows_placed")
        s_xTp, s_xTh, s_xTl = sem("xT_in_psum"), sem("xT_hi"), sem("xT_lo")
        s_qp, s_qh, s_ql = sem("q_in_psum"), sem("q_hi"), sem("q_lo")
        s_sn, s_mx = sem("scores_for_max"), sem("max_taken")
        s_nmh, s_nm = sem("negmax_hi"), sem("negmax_split")
        s_nTp, s_nT, s_nrow = sem("negmaxT_in_psum"), sem("negmaxT_copied"), sem("negmax_rows_placed")
        s_st, s_e = sem("scoresT_in_psum"), sem("exp_done")
        s_o, s_dn, s_osb = sem("pv_in_psum"), sem("denominators_in_psum"), sem("pv_copied")
        s_rd, s_bc, s_oT = sem("denominators_inverted"), sem("inverse_spread"), sem("attn_normalised")
        s_wo, s_x1 = sem("wo_in_psum"), sem("x1_done")
        s_x2p, s_x2T = sem("x2T_in_psum"), sem("x2T_copied")
        s_early1, s_early2, s_early, s_earlyh = sem("early_one_term"), sem("early_two_terms"), sem("early_mixed"), sem("early_hi")
        s_mix1, s_mix2, s_xm = sem("mix_one_term"), sem("mix_two_terms"), sem("mixed")
        s_xmh, s_xml = sem("mixed_hi"), sem("mixed_lo")
        s_f, s_fa, s_fv = sem("ffn_slot_filled"), sem("ffn_slot_read_by_act"), sem("ffn_slot_read_by_dve")
        s_gmax, s_gcand, s_gidx, s_oh = sem("gate_max"), sem("gate_cand"), sem("gate_index"), sem("onehot")
        s_x1b, s_yg, s_yo = sem("x1_plus_beta"), sem("times_gamma"), sem("out_ready")
        s_lf, s_lfa, s_lfv = sem("last_ffn_filled"), sem("last_ffn_read_by_act"), sem("last_ffn_read_by_dve")
        s_lhh, s_lhl, s_lones = sem("last_selected_hi"), sem("last_selected_lo"), sem("last_b2_selector_ones")
        s_lyg, s_lx1b, s_lyo = sem("last_times_gamma"), sem("last_x1_plus_beta"), sem("last_out_ready")
        s_xh2f, s_hh, s_hl = sem("xh2_kept"), sem("selected_hi"), sem("selected_lo")
        s_out = [sem(f"out_stored{j}") for j in range(NJ)]

        def at(b, per_row, n):
            return b * per_row + n

        xr = x.rearrange("b (j k p) d -> p b j k d", p=P, k=NT)
        outr = out.rearrange("b (j k p) d -> p b j k d", p=P, k=NT)
        mr = mask.rearrange("b o (j k p) s -> p (b o) j k s", p=P, k=NT)

        def halves(par):
            return (slice(0, 64), slice(64, 128)) if par == 0 else (slice(64, 128), slice(0, 64))

        def banks_for_max(n, f):
            return (6, 2) if n and not f else (2, 4)

        def row_broadcast(vec, n, parts=P):
            return vec.rearrange("(o n) -> o n", o=1).broadcast_to([parts, n])

        NFA, NFV, NU = NM, NM + 3, 2 * NM + 3

        class Path:

            def __init__(self, filled, read_by_act, read_by_dve, hi_done, lo_done):
                self.s_f, self.s_fa, self.s_fv, self.s_hh, self.s_hl = filled, read_by_act, read_by_dve, hi_done, lo_done

            def filled(self, b, j, use):
                return self.count(b, j, NU, self.uses.index(use) + 1)

            def read_by_act(self, b, j, n):
                return self.count(b, j, NFA, n)

            def read_by_dve(self, b, j, n):
                return self.first + self.count(b, j, NFV, n)

        class Usual(Path):
            uses = ["h0", "h4", "h1", "gate", "h2", "h3", "rep0", "rep1", "rep2", "rep3", "rep4", "w2a", "w2b"]
            by_act = [u in ("h4", "h0", "h1", "h2", "h3") for u in uses]
            first = 1
            tanh = 2

            def count(self, b, j, per, n):
                return at(b, NJ * per, j * per + n)

            def bank(self, j, use):
                return 6 + (j * NU + self.uses.index(use)) % 2

            def h(self, m, rows=slice(0, P)):
                return hs[rows, m, :]

            def selected(self, m, r):
                return hs[0:r, m, :] if m < 4 else h4s[0:r, :]

            def hi(self, m, r):
                return hmh[0:r, m, :]

            def lo(self, m, r):
                return hml[0:r, m, :]

            def x(self, k):
                return xh2f[:, k, :]

        class Last(Path):
            uses = ["h4", "h0", "h1", "gate", "h2", "h3", "rep0", "rep1", "rep2", "rep3", "rep4", "w2a", "w2b"]
            banks = {"h4": 4, "h0": 0, "h1": 1, "h2": 2, "h3": 3, "gate": 5, "rep0": 0, "rep1": 1, "rep2": 2, "rep3": 3,
                     "rep4": 4, "w2a": 5, "w2b": 0}
            first = 0
            tanh = 1

            def count(self, b, j, per, n):
                return n

            def bank(self, j, use):
                return self.banks[use]

            def h(self, m, rows=slice(0, P)):
                return e[rows, m, :]

            def selected(self, m, r):
                return e[0:r, m, :] if m < 4 else e[0:r, 5, :]

            def hi(self, m, r):
                return qh[0:r, m, :] if m < 4 else xTh[0:r, 0, :]

            def lo(self, m, r):
                return ql[0:r, m, :] if m < 4 else xTl[0:r, 0, :]

            def x(self, k):
                return xh2[:, 1, k, :]

        usual, last = Usual(s_f, s_fa, s_fv, s_hh, s_hl), Last(s_lf, s_lfa, s_lfv, s_lhh, s_lhl)
        last_y = xin[:, 1]

        def rows_of(m):
            return P if m < 4 else DM + NPATH

        block = stack.enter_context(nc.Block())

        @block.sync
        def _(sp):
            def load(dst, src, s):
                sp.dma_start(dst, src).then_inc(s, 16)

            load(ident, consts[:, C_ID:C_ID + P], s_ident)
            load(xin[:, 0], xr[:, 0, 0], s_x[0])
            load(min_[:, 0], mr[:, 0, 0], s_m[0])
            load(cst[:, C_D4:C_E], consts[:, C_D4:C_E], s_rows)

            def twice(rows):
                return rows.rearrange("p (o t) -> p o t", o=1).broadcast_to([rows.shape[0], 2, CH])

            def place_mask(b, j):
                sp.wait_ge(s_st, at(b, NJ * NPAIR, j * NPAIR))
                sp.wait_ge(s_mT, at(b, NJ, j + 1))
                for par in range(2):
                    _, mrow = halves(par)
                    sp.dma_start(qh[mrow, par::2, :].bitcast(F32), twice(mT[mrow, :])).then_inc(s_mrow, 16)

            def place_maxima(b, j):
                sp.wait_ge(s_nT, at(b, NJ, j + 1))
                for par in range(2):
                    r0 = halves(par)[1].start
                    sp.dma_start(ql[r0:r0 + 32, par::2, :].bitcast(F32), twice(nmT)).then_inc(s_nrow, 16)

            def next_inputs(b, j):
                sp.wait_ge(s_ln1, at(b, NJ, j + 1))
                sp.wait_ge(s_xb, at(b, NJ, j + 1))
                sp.dma_start(xin[:, j], xr[:, b + 1, j]).then_inc(s_x[j], 16)
                sp.wait_ge(s_mb, at(b, NJ, j + 1))
                sp.dma_start(min_[:, j], mr[:, b + 1, j]).then_inc(s_m[j], 16)

            def store(b, j):
                sp.wait_ge(s_yo, 1 + at(b, NJ, j + 1))
                sp.dma_start(outr[:, b, j], y[:, :, :]).then_inc(s_out[j], 16)

            def row(r, feed_forward, more):
                for j in range(NJ):
                    front = (r, 1) if j == 0 else (r + 1, 0)
                    if more and not feed_forward:
                        next_inputs(r, j)
                    if j == 0 or more:
                        place_mask(*front)
                    if more and feed_forward:
                        next_inputs(r, j)
                    if not feed_forward and j == 0:
                        load_ffn_weights()
                    if j == 0 or more:
                        place_maxima(*front)
                    if feed_forward:
                        store(r - 1, j)

            def load_ffn_weights():
                for c in range(KD):
                    load(w1_32[:, c, 0:NPATH * DM].rearrange("p (n m) -> p n m", n=NPATH),
                         W1[:, c * P:(c + 1) * P, :].rearrange("n p m -> p n m"), s_wf)
                load(w1_32[:, :, NPATH * DM:], Wo1.rearrange("(c p) m -> p c m", p=P), s_wf)
                load(w2_32[:, 0:4, :], W2[0:8].rearrange("(t a) m d -> (a m) t d", a=2), s_wf)
                load(w2_32[0:DM, 4, :], W2[8], s_wf)
                load(w2_32[DM:DM + NPATH, 4, :], b2, s_wf)
                load(wo2[DM:, :], Wo2, s_wf)
                load(b1s[:, 0:4], b1[0:8].rearrange("(t a) m -> (a m) t", a=2), s_wf)
                load(b1s[0:DM, 4:5], b1[8].rearrange("(m o) -> m o", o=1), s_wf)
                load(b1s[DM:, 4:5], bo1.rearrange("(m o) -> m o", o=1), s_wf)
                load(bo2s[:, :], row_broadcast(bo2, NPATH), s_wf)
                load(mks[:, :, :], mixk.rearrange("t (c p) -> p t c", p=P), s_wf)
                load(gms[:, :], row_broadcast(gamma, D), s_wf)
                load(bts[:, :], row_broadcast(beta, D), s_wf)

            place_mask(0, 0)
            load(xin[:, 1], xr[:, 0, 1], s_x[1])
            load(min_[:, 1], mr[:, 0, 1], s_m[1])
            load(cst[:, C_E:], consts[:, C_E:], s_cst)
            load(bos[:, :], row_broadcast(bo, D), s_wo_in)
            load(wo[:, :, :], Wo.rearrange("(c p) n -> p c n", p=P), s_wo_in)
            place_maxima(0, 0)
            row(0, False, True)
            with sp.Fori(1, B - 1) as r:
                row(r, True, True)
            row(B - 1, True, False)
            store(B - 1, 0)
            for half in range(2):
                sp.wait_ge(s_lyo, half + 1)
                h = slice(2 * half, 2 * half + 2)
                sp.dma_start(outr[:, B - 1, 1, h], last_y[:, h, :]).then_inc(s_out[1], 16)
            sp.wait_ge(s_out[0], 16 * B)
            sp.wait_ge(s_out[1], 16 + 16 * (B - 1) + 32)

        @block.tensor
        def _(pe):
            def two_pass(out_, lhs, rhs):
                for i in range(2):
                    for k in range(KD):
                        nc.tensor.matmul(out_, lhs[i](k), rhs(k), start=(i == 0 and k == 0), stop=False)

            def third_pass(out_, lhs, rhs):
                for k in range(KD):
                    mm = nc.tensor.matmul(out_, lhs(k), rhs(k), start=False, stop=(k == KD - 1))
                return mm

            def context_transposed():
                pe.wait_ge(s_ident, 16)
                pe.wait_ge(s_ctx, 16)
                for b in range(B):
                    for k in range(KD):
                        i = (k * B + b) * SK
                        mm = nc.tensor.transpose(ps[:, 3, i:i + SK], ctx_in[:, b, k * P:(k + 1) * P], ident[0:SK, 0:SK])
                mm.then_inc(s_setup_pe, 1)

            def keys():
                pe.wait_ge(s_setup_v, 2)
                pe.wait_ge(s_wk, 16 * WK_LOADS)
                for k in range(KD):
                    mm = nc.tensor.matmul(ps[:, 4, 0:B * SK].rearrange("p (b s) -> p b s", b=B), wk8[:, k, :],
                                          ctxT[:, k, :, 0, :], start=(k == 0), stop=(k == KD - 1))
                mm.then_inc(s_setup_pe, 1)

            def values():
                for b in range(B):
                    for k in range(KD):
                        mm = nc.tensor.matmul(ps[:, 1, b * DK:(b + 1) * DK], ctxT[:, k, b, :, :], wv[:, k, :],
                                              start=(k == 0), stop=(k == KD - 1))
                mm.then_inc(s_setup_pe, 1)

            def t1(b, j, bank):
                pe.wait_ge(s_mb, at(b, NJ, j + 1))
                pe.wait_ge(s_mx, at(b, NJ * NT, j * NT))
                for k in range(NT):
                    mm = nc.tensor.transpose(ps_b[:, k * P:(k + 1) * P], mb[:, k, :, :], ident_b[:, :])
                mm.then_inc(s_mTp, 1)
                pe.wait_ge(s_ln1, at(b, NJ, j + 1))
                pe.wait_ge(s_nT, at(b, NJ, j))
                pe.wait_ge(s_ql, at(b, NJ, j))
                for c in range(KD):
                    if bank == 0:
                        pe.wait_ge(s_x2T, at(b, NJ * KD, (j - 2) * KD + c + 1))
                    for k in range(NT):
                        mm = nc.tensor.transpose(ps[:, bank + c, k * P:(k + 1) * P], xh1[:, k, c * P:(c + 1) * P], ident)
                    mm.then_inc(s_xTp, 1)

            def wq(b, j, bank):
                pe.wait_ge(s_xTl, at(b, NJ, j + 1))
                for m in range(KD):
                    ms = slice(m * P, (m + 1) * P)
                    two_pass(ps[:, bank + m, :], (lambda k: wqh[:, k, ms], lambda k: wql[:, k, ms]), lambda k: xTh[:, k, :])
                    third_pass(ps[:, bank + m, :], lambda k: wqh[:, k, ms], lambda k: xTl[:, k, :]).then_inc(s_qp, 1)

            def scores_for_max(b, j, k, banks):
                if k == 0:
                    pe.wait_ge(s_qh, at(b, NJ, j + 1))
                    pe.wait_ge(s_mrow, at(b, 32 * NJ, 32 * (j + 1)))
                    pe.wait_ge(s_km, at(b, 3, 2))
                    pe.wait_ge(s_mT, at(b, NJ, j + 1))
                if banks[k % 2] == 2 and k < 2:
                    pe.wait_ge(s_rd, at(b, NJ, j))
                if banks[k % 2] == 4 and k < 2:
                    pe.wait_ge(s_oT, at(b, NJ, j))
                if banks[k % 2] == 6 and k < 2:
                    pe.wait_ge(s_ql, at(b, NJ, j + 1))
                if k >= 2:
                    pe.wait_ge(s_mx, at(b, NJ * NT, j * NT + k - 1))
                for q in range(NQ):
                    bank = banks[k % 2] + q // 2
                    mm = nc.tensor.matmul(ps[:, bank, (q % 2) * 256:(q % 2 + 1) * 256],
                                          qh[:, q, k * P:(k + 1) * P], kmh[:, q % 2, :],
                                          start=True, stop=True)
                mm.then_inc(s_sn, 1)

            def negmax_transposed(b, j, bank, n):
                pe.wait_ge(s_nm, at(b, NJ, j + 1))
                if n:
                    pe.wait_ge(s_ql, at(b, NJ, j + 1))
                if bank == 0 and n:
                    pe.wait_ge(s_x1, at(b, 2 * NJ, 2 * j))
                for k in range(NT):
                    mm = nc.tensor.transpose(ps[0:32, bank, k * P:(k + 1) * P], nm[:, k, :].bitcast(F32), ident)
                mm.then_inc(s_nTp, 1)

            def scores_transposed(b, j, front):
                if front:
                    pe.wait_ge(s_mT, at(b, NJ, j + 2))
                pe.wait_ge(s_ql, at(b, NJ, j + 1))
                pe.wait_ge(s_nrow, at(b, 32 * NJ, 32 * (j + 1)))
                pe.wait_ge(s_mx, at(b, NJ * NT, (j + 1) * NT))
                for p in range(NPAIR):
                    q, c = p // 2, slice((p % 2) * P, (p % 2 + 1) * P)
                    bank = 2 + p % 4
                    if p >= 4 and p % 2 == 0:
                        pe.wait_ge(s_e, at(b, NJ * 4, j * 4 + p // 2 - 1))
                    nc.tensor.matmul(ps[:, bank, :], kmh[:, q % 2, c], qh[:, q, :], start=True, stop=False)
                    nc.tensor.matmul(ps[:, bank, :], kml[:, q % 2, c], qh[:, q, :], start=False, stop=False)
                    nc.tensor.matmul(ps[:, bank, :], kms[:, q, c], ql[:, q, :],
                                     start=False, stop=True).then_inc(s_st, 1)

            def pv(b, j, front, f):
                pe.wait_ge(s_km, at(b, 3, 3))
                if front and f:
                    pe.wait_ge(s_ql, at(b, NJ, j + 2))
                else:
                    pe.wait_ge(s_x2T, at(b, NJ * KD, j * KD))
                for half in range(2):
                    pe.wait_ge(s_e, at(b, NJ * 4, j * 4 + 2 * half + 2))
                    for p in range(4):
                        mm = nc.tensor.matmul(ps[32 * p:32 * p + 32, half, :], vd[:, :], e[:, 4 * half + p, :],
                                              start=True, stop=True)
                mm.then_inc(s_o, 1)
                for p in range(NPAIR):
                    for k in range(NT):
                        mm = nc.tensor.matmul(ps[32 * k:32 * k + 32, 2, 0:P], cst[:, C_E + 32 * p:C_E + 32 * p + 32],
                                              e[:, p, k * P:(k + 1) * P], start=(p == 0), stop=(p == NPAIR - 1))
                mm.then_inc(s_dn, 1)

            def spread(b, j):
                pe.wait_ge(s_rd, at(b, NJ, j + 1))
                for c in range(KD):
                    for k in range(NT):
                        w = C_BC + (c * NT + k) * P
                        mm = nc.tensor.matmul(ps[:, 4 + c, k * P:(k + 1) * P], cst[:, w:w + P], rD[:, :],
                                              start=True, stop=True)
                mm.then_inc(s_bc, 1)

            def project_out(b, j, tiles):
                if tiles[0] == 0:
                    pe.wait_ge(s_osb, at(b, NJ, j + 1))
                    pe.wait_ge(s_oT, at(b, NJ, j + 1))
                for k in tiles:
                    for c in range(KD):
                        mm = nc.tensor.matmul(ps[:, k // 2, (k % 2) * D:(k % 2 + 1) * D], osb[:, c, k * P:(k + 1) * P],
                                              wo[:, c, :], start=(c == 0), stop=(c == KD - 1))
                mm.then_inc(s_wo, 1)

            def t2(b, j, front):
                if front:
                    pe.wait_ge(s_nT, at(b, NJ, j + 2))
                pe.wait_ge(s_ln2, at(b, NJ, j + 1))
                for c in range(KD):
                    for k in range(NT):
                        mm = nc.tensor.transpose(ps[:, c, k * P:(k + 1) * P], xh2[:, j, k, c * P:(c + 1) * P], ident)
                    mm.then_inc(s_x2p, 1)

            def take_slot(b, j, use, L):
                if L is last:
                    if use == "h4":
                        pe.wait_ge(s_x2T, at(b, NJ * KD, NJ * KD))
                        pe.wait_ge(s_oT, at(b, NJ, NJ))
                    elif use[:3] == "rep":
                        pe.wait_ge(L.s_fa, min(int(use[3]) + 2, NFA))
                    elif use == "w2a":
                        pe.wait_ge(L.s_fv, 1)
                    elif use == "w2b":
                        pe.wait_ge(L.s_fv, 2)
                else:
                    before = j * NU + L.uses.index(use) - 2
                    if before < 0:
                        pe.wait_ge(L.s_fv, L.read_by_dve(b, 0, 0))
                    else:
                        act = L.by_act[before % NU]
                        reads = sum(L.by_act[i % NU] == act for i in range(before + 1))
                        if act:
                            pe.wait_ge(L.s_fa, at(b, NJ * NFA, reads))
                        else:
                            pe.wait_ge(L.s_fv, L.first + at(b, NJ * NFV, reads))
                return ps[:, L.bank(j, use), :]

            def w1(b, j, m, L=usual):
                o = take_slot(b, j, f"h{m}", L)
                js, ms = slice(j * CH, (j + 1) * CH), slice(m * P, (m + 1) * P)
                pe.wait_ge(s_xmh, at(b, NJ * KD, (j + 1) * KD))
                two_pass(o, (lambda k: w1h[:, k, ms], lambda k: w1l[:, k, ms]), lambda k: xmh[:, k, js])
                pe.wait_ge(s_xml, at(b, NJ * KD, (j + 1) * KD))
                third_pass(o, lambda k: w1h[:, k, ms], lambda k: xml[:, k, js]).then_inc(L.s_f, 1)

            def gate(b, j, L=usual):
                o = take_slot(b, j, "gate", L)
                pe.wait_ge(L.s_fa, L.read_by_act(b, j, L.tanh))
                for k in range(NT):
                    mm = nc.tensor.matmul(o[:, k * NPATH:(k + 1) * NPATH], thT[DM:, k * P:(k + 1) * P],
                                          wo2[DM:, :], start=True, stop=True)
                mm.then_inc(L.s_f, 1)

            def rep(b, j, m, L=usual):
                o = take_slot(b, j, f"rep{m}", L)
                if m == 0:
                    pe.wait_ge(s_oh, at(b, NJ, j + 1))
                for k in range(NT):
                    ks = slice(k * P, (k + 1) * P)
                    for a in range(2):
                        p = 2 * m + a
                        if p < NPATH:
                            sel = oh[:, k, p:p + 1].broadcast_to([P, DM])
                            mm = nc.tensor.matmul(o[a * DM:(a + 1) * DM, ks], sel, ident_b[:, :], start=True, stop=True)
                        else:
                            mm = nc.tensor.matmul(o[DM:DM + NPATH, ks], oh[:, k, 0:NPATH], ident_b[:, :],
                                                  start=True, stop=True)
                mm.then_inc(L.s_f, 1)

            def w2_product(b, j, k, terms, L=usual):
                if k % 2 == 0 and terms == "hi":
                    take_slot(b, j, ("w2a", "w2b")[k // 2], L)
                o = ps[:, L.bank(j, ("w2a", "w2b")[k // 2]), (k % 2) * D:(k % 2 + 1) * D]
                ks = slice(k * P, (k + 1) * P)
                for m in range(NM):
                    r = rows_of(m)
                    if terms == "hi":
                        if k == 0:
                            pe.wait_ge(L.s_hh, L.count(b, j, NM, m + 1))
                        nc.tensor.matmul(o, L.hi(m, r)[:, ks], w2h[0:r, m, :], start=(m == 0), stop=False)
                        nc.tensor.matmul(o, L.hi(m, r)[:, ks], w2l[0:r, m, :], start=False, stop=False)
                    else:
                        if k == 0:
                            pe.wait_ge(L.s_hl, L.first + L.count(b, j, NM, m + 1))
                        mm = nc.tensor.matmul(o, L.lo(m, r)[:, ks], w2h[0:r, m, :], start=False, stop=(m == NM - 1))
                if k % 2 == 1 and terms == "lo":
                    mm.then_inc(L.s_f, 1)

            def w2_tiles(b, j, tiles, L=usual):
                for k in tiles:
                    w2_product(b, j, k, "hi", L)
                    w2_product(b, j, k, "lo", L)

            def step(n, front, f, after):
                banks = banks_for_max(n, f)
                fb = 0 if f else 6
                if n:
                    scores_transposed(*n, front)
                if front:
                    wq(*front, fb)
                if f:
                    w1(*f, 0)
                    w1(*f, 4)
                    w1(*f, 1)
                    gate(*f)
                if n:
                    pv(*n, front, f)
                if f:
                    w1(*f, 2)
                    w1(*f, 3)
                    rep(*f, 0)
                elif front:
                    scores_for_max(*front, 0, banks)
                    scores_for_max(*front, 1, banks)
                if n:
                    spread(*n)
                if f:
                    rep(*f, 1)
                    if front:
                        scores_for_max(*front, 0, banks)
                    rep(*f, 2)
                    if front:
                        scores_for_max(*front, 1, banks)
                elif front:
                    scores_for_max(*front, 2, banks)
                    scores_for_max(*front, 3, banks)
                if n:
                    project_out(*n, (0, 1))
                if f:
                    rep(*f, 3)
                    if front:
                        scores_for_max(*front, 2, banks)
                    rep(*f, 4)
                if n:
                    project_out(*n, (2, 3))
                if f and front:
                    scores_for_max(*front, 3, banks)
                if f:
                    w2_tiles(*f, (0, 1))
                if front:
                    negmax_transposed(*front, fb if n else 0, n)
                if f:
                    w2_tiles(*f, (2, 3))
                if after and not f:
                    t1(*after, 6)
                if n:
                    t2(*n, front)
                if after and f:
                    t1(*after, 0)

            context_transposed()
            keys()
            pe.wait_ge(s_id, 1)
            t1(0, 0, 6)
            values()
            pe.wait_ge(s_wqh, 1)
            pe.wait_ge(s_wql, 1)
            step(None, (0, 0), None, (0, 1))
            pe.wait_ge(s_cst, 16)
            pe.wait_ge(s_wo_in, 32)
            step((0, 0), (0, 1), None, (1, 0))
            step((0, 1), (1, 0), None, (1, 1))
            for done in (s_w1h, s_w1l, s_w2h, s_w2l):
                pe.wait_ge(done, 1)
            with pe.Fori(1, B - 1) as r:
                step((r, 0), (r, 1), (r - 1, 0), (r + 1, 0))
                step((r, 1), (r + 1, 0), (r - 1, 1), (r + 1, 1))
            step((B - 1, 0), (B - 1, 1), (B - 2, 0), None)
            step((B - 1, 1), None, (B - 2, 1), None)
            f0, f1 = (B - 1, 0), (B - 1, 1)
            w1(*f0, 0)
            w1(*f0, 4)
            w1(*f0, 1)
            gate(*f0)
            w1(*f0, 2)
            w1(*f0, 3)
            rep(*f0, 0)
            rep(*f0, 1)
            w1(*f1, 4, last)
            rep(*f0, 2)
            w1(*f1, 0, last)
            rep(*f0, 3)
            w1(*f1, 1, last)
            rep(*f0, 4)
            gate(*f1, last)
            w1(*f1, 2, last)
            w1(*f1, 3, last)
            for m in range(NM):
                rep(*f1, m, last)
            w2_tiles(*f0, range(NT))
            w2_tiles(*f1, range(NT), last)

        @block.scalar
        def _(act):
            def load(dst, src, s):
                act.dma_start(dst, src).then_inc(s, 16)

            load(ctx_in, ctx.rearrange("b s d -> s b d"), s_ctx)
            load(wk[:, :, :], Wk.rearrange("(c p) n -> p c n", p=P), s_wk)
            load(wv[:, :, :], Wv.rearrange("(c p) n -> p c n", p=P), s_wk)
            load(bks[:, :], bk.rearrange("(h p o) -> h p o", h=1, o=1).broadcast_to([P // DK, DK, 1]), s_wk)
            load(bvs[:, :], row_broadcast(bv, DK), s_wk)
            load(wq32, Wq.rearrange("(c p) n -> p c n", p=P), s_wq)
            load(bqs[:, :], bq.rearrange("(c p) -> p c", p=P), s_wq)

            def wq_high():
                act.wait_ge(s_wq, 32)
                nc.scalar.activation(wqh[:, :, :], wq32, ACT.Copy).then_inc(s_wqh, 1)

            def split_ffn_weights():
                act.wait_ge(s_wf, 16 * WF_LOADS)
                nc.scalar.activation(w1h[:, :, :], w1_32, ACT.Copy).then_inc(s_w1h, 1)
                nc.scalar.activation(w2h[:, 0:4, :], w2_32[:, 0:4, :], ACT.Copy)
                r = DM + NPATH
                nc.scalar.activation(w2h[0:r, 4, :], w2_32[0:r, 4, :], ACT.Copy).then_inc(s_w2h, 1)

            def copies_t1(b, j, bank):
                act.wait_ge(s_mTp, at(b, NJ, j + 1))
                act.wait_ge(s_mrow, at(b, 32 * NJ, 32 * j))
                nc.scalar.activation(mT[:, :], ps_b, ACT.Copy).then_inc(s_mT, 1)
                act.wait_ge(s_qp, at(b, NJ * KD, j * KD))
                for c in range(KD):
                    act.wait_ge(s_xTp, at(b, NJ * KD, j * KD + c + 1))
                    nc.scalar.activation(xTh[:, c, :], ps[:, bank + c, :], ACT.Copy).then_inc(s_xTh, 1)

            def q_hi(b, j, bank):
                act.wait_ge(s_st, at(b, NJ * NPAIR, j * NPAIR))
                for m in range(KD):
                    act.wait_ge(s_qp, at(b, NJ * KD, j * KD + m + 1))
                    for par in range(2):
                        r, _ = halves(par)
                        a = nc.scalar.activation(qh[r, 2 * m + par, :], ps[r, bank + m, :], ACT.Identity, bias=bqs[r, m:m + 1])
                a.then_inc(s_qh, 1)

            def maxima(b, j, bank):
                act.wait_ge(s_nTp, at(b, NJ, j + 1))
                act.wait_ge(s_nrow, at(b, 32 * NJ, 32 * j))
                nc.scalar.activation(nmT, ps[0:32, bank, :], ACT.Copy).then_inc(s_nT, 1)

            def softmax_exp(b, j):
                act.wait_ge(s_dn, at(b, NJ, j))
                for i in range(4):
                    act.wait_ge(s_st, at(b, NJ * NPAIR, j * NPAIR + 2 * i + 2))
                    bank = 2 + 2 * (i % 2)
                    nc.scalar.activation(e[:, 2 * i:2 * i + 2, :], ps[:, bank:bank + 2, :], ACT.Exp).then_inc(s_e, 1)

            def pv_copy(b, j):
                act.wait_ge(s_o, at(b, NJ, j + 1))
                act.wait_ge(s_wo, at(b, 2 * NJ, 2 * j))
                nc.scalar.activation(osb[:, :, :], ps[:, 0:2, :], ACT.Copy).then_inc(s_osb, 1)

            def copy_t2(b, j):
                act.wait_ge(s_xm, at(b, NJ * KD, 0))
                for c in range(KD):
                    act.wait_ge(s_x2p, at(b, NJ * KD, j * KD + c + 1))
                    nc.scalar.activation(x2T[:, c, 1 + j * CH:1 + (j + 1) * CH], ps[:, c, :], ACT.Copy).then_inc(s_x2T, 1)

            def layernorm1_apply(b, j):
                act.wait_ge(s_xTp, at(b, NJ * KD, j * KD))
                act.wait_ge(s_ln1b, at(b, NJ, j + 1))
                for k in range(NT):
                    a = nc.scalar.activation(xh1[:, k, :], xin[:, j, k, :], ACT.Identity,
                                             bias=ln1[5][:, k:k + 1], scale=ln1[7][:, k:k + 1])
                a.then_inc(s_ln1, 1)

            def mixed_hi(b, j, first=0):
                for c in range(KD):
                    act.wait_ge(s_xm, at(b, NJ * KD, j * KD + c + 1))
                    nc.scalar.activation(xmh[:, c, j * CH + first:(j + 1) * CH], xm[:, c, first:], ACT.Copy).then_inc(s_xmh, 1)

            def early_mixed_hi():
                for c in range(KD):
                    act.wait_ge(s_early, c + 1)
                    nc.scalar.activation(xmh[:, c, 0:CH - 1], xm[:, c, 0:CH - 1], ACT.Copy).then_inc(s_earlyh, 1)

            def hidden(b, j, m, L=usual):
                act.wait_ge(L.s_f, L.filled(b, j, f"h{m}"))
                bank = L.bank(j, f"h{m}")
                if L is usual and m == 0:
                    act.wait_ge(s_hl, 1 + at(b, NJ * NM, j * NM))
                if m == 4:
                    if L is last:
                        act.wait_ge(s_dn, at(b, NJ, NJ))
                        act.wait_ge(s_f, usual.filled(b, 0, "gate"))
                    nc.scalar.activation(L.h(4, slice(0, DM)), ps[0:DM, bank, :], ACT.Identity, bias=b1s[0:DM, 4:5])
                    nc.scalar.activation(thT[DM:, :], ps[DM:, bank, :], ACT.Tanh, bias=b1s[DM:, 4:5]).then_inc(L.s_fa, 1)
                else:
                    nc.scalar.activation(L.h(m), ps[:, bank, :], ACT.Identity, bias=b1s[:, m:m + 1]).then_inc(L.s_fa, 1)

            def keep_xh2(b, j):
                act.wait_ge(s_yg, 1 + at(b, NJ, j))
                nc.scalar.activation(xh2f[:, :, :], xh2[:, j], ACT.Copy).then_inc(s_xh2f, 1)

            def selected_hi(b, j, m, L=usual):
                act.wait_ge(L.s_fv, L.read_by_dve(b, j, m + 2))
                r = rows_of(m)
                nc.scalar.activation(L.hi(m, r), L.selected(m, r), ACT.Copy).then_inc(L.s_hh, 1)

            def step(n, front, f, after):
                if n:
                    softmax_exp(*n)
                if f and f[1] == 0:
                    mixed_hi(*f)
                if front:
                    q_hi(*front, 0 if f else 6)
                if f:
                    hidden(*f, 0)
                    hidden(*f, 4)
                if n and not front:
                    early_mixed_hi()
                if f:
                    hidden(*f, 1)
                if n:
                    pv_copy(*n)
                if f:
                    hidden(*f, 2)
                    hidden(*f, 3)
                if f and f[1] == 0:
                    mixed_hi(f[0], 1)
                if f:
                    keep_xh2(*f)
                if f:
                    for m in range(NM):
                        selected_hi(*f, m)
                if after:
                    layernorm1_apply(*after)
                if n and n[1] == 0 and not f:
                    split_ffn_weights()
                if front:
                    maxima(*front, 0 if f or not n else 6)
                if after and not f:
                    copies_t1(*after, 6)
                if n:
                    copy_t2(*n)
                if n and not front:
                    mixed_hi(n[0], 0, CH - 1)
                if after and f:
                    copies_t1(*after, 0)

            act.wait_ge(s_init, 1)
            nc.scalar.activation(tables[:, :], halfneg[:, :], ACT.Exp)
            wq_high()
            layernorm1_apply(0, 0)
            copies_t1(0, 0, 6)
            step(None, (0, 0), None, (0, 1))
            step((0, 0), (0, 1), None, (1, 0))
            step((0, 1), (1, 0), None, (1, 1))
            act.wait_ge(s_w1l, 1)
            act.wait_ge(s_w2l, 1)
            act.wait_ge(s_ones, 1)
            with act.Fori(1, B - 1) as r:
                step((r, 0), (r, 1), (r - 1, 0), (r + 1, 0))
                step((r, 1), (r + 1, 0), (r - 1, 1), (r + 1, 1))
            step((B - 1, 0), (B - 1, 1), (B - 2, 0), None)
            step((B - 1, 1), None, (B - 2, 1), None)
            f0, f1 = (B - 1, 0), (B - 1, 1)
            hidden(*f0, 0)
            hidden(*f0, 4)
            hidden(*f0, 1)
            mixed_hi(*f1)
            hidden(*f0, 2)
            hidden(*f0, 3)
            keep_xh2(*f0)
            selected_hi(*f0, 0)
            hidden(*f1, 4, last)
            selected_hi(*f0, 1)
            hidden(*f1, 0, last)
            selected_hi(*f0, 2)
            hidden(*f1, 1, last)
            selected_hi(*f0, 3)
            selected_hi(*f0, 4)
            hidden(*f1, 2, last)
            hidden(*f1, 3, last)
            for m in range(NM):
                selected_hi(*f1, m, last)

        @block.vector
        def _(dve):
            v = nc.vector

            def memsets():
                v.memset(x2T[:, :, 0:1], 0.0).then_inc(s_fv, 1)
                v.memset(x2T[:, :, S + 1:S + 2], 0.0)
                v.memset(oh[:, :, :], 0.0)

            def transposed_context_copied():
                dve.wait_ge(s_setup_pe, 1)
                for a in range(2):
                    ins = v.tensor_copy(ctxT[:, :, :, a, :], ps[:, 3, :].rearrange("p (c b s) -> p c b s", c=KD, b=B))
                ins.then_inc(s_setup_v, 1)

            def key_weights_repeated():
                dve.wait_ge(s_wk, 16 * WK_LOADS)
                v.tensor_copy(wk8[:, :, :].rearrange("p c (h d) -> p c h d", h=8),
                              wk[:, :, :].rearrange("p c (h d) -> p c h d", h=1).broadcast_to([P, KD, 8, DK])).then_inc(s_setup_v, 1)

            def keys():
                dve.wait_ge(s_setup_pe, 2)
                v.tensor_scalar(krep[:, :, :], ps[:, 4, 0:B * SK].rearrange("p (b s) -> p b s", b=B), bks[:, 0:1],
                                float(DK) ** -0.5, ALU.add, ALU.mult).then_inc(s_setup_v, 1)
                dve.wait_ge(s_setup_v, 3)
                v.tensor_copy(khi[:, :, :], krep[:, :, :]).then_inc(s_setup_v, 1)
                dve.wait_ge(s_setup_v, 4)
                v.tensor_tensor(klo[:, :, :], krep[:, :, :], khi[:, :, :].bitcast(F32), ALU.subtract).then_inc(s_setup_v, 1)

            def values():
                dve.wait_ge(s_setup_pe, 3)
                v.tensor_tensor(vall[:, :, :], ps[:, 1, 0:B * DK].rearrange("p (b d) -> p b d", b=B),
                                bvs[:, :].rearrange("p (b d) -> p b d", b=1).broadcast_to([P, B, DK]),
                                ALU.add).then_inc(s_setup_v, 1)

            def constant_rows():
                dve.wait_ge(s_rows, 16)
                for q in range(NQ):
                    _, m = halves(q % 2)
                    v.tensor_copy(kms[m, q, :], cst[m, C_SEL + q * 256:C_SEL + (q + 1) * 256])
                for par in range(2):
                    _, m = halves(par)
                    a = v.tensor_copy(kmh[m, par, :], cst[m, C_IDK:C_IDK + 256])
                a.then_inc(s_kc, 1)

            def wq_lo():
                dve.wait_ge(s_wqh, 1)
                v.tensor_tensor(wql[:, :, :], wq32, wqh[:, :, :].bitcast(F32), ALU.subtract).then_inc(s_wql, 1)

            def ffn_weights_lo():
                dve.wait_ge(s_w1h, 1)
                v.tensor_tensor(w1l[:, :, :], w1_32, w1h[:, :, :].bitcast(F32), ALU.subtract).then_inc(s_w1l, 1)
                dve.wait_ge(s_w2h, 1)
                v.tensor_tensor(w2l[:, 0:4, :], w2_32[:, 0:4, :], w2h[:, 0:4, :].bitcast(F32), ALU.subtract)
                r = DM + NPATH
                v.tensor_tensor(w2l[0:r, 4, :], w2_32[0:r, 4, :], w2h[0:r, 4, :].bitcast(F32),
                                ALU.subtract).then_inc(s_w2l, 1)
                dve.wait_ge(s_w2l, 1)
                v.memset(hs[DM:, 4, :], 1.0).then_inc(s_ones, 1)

            def last_finish(b, j):
                c = at(b, NJ, j + 1)
                dve.wait_ge(s_ln3v, c)
                for k in range(NT):
                    a = v.scalar_tensor_tensor(out=last_y[:, k, :], in0=last.x(k), scalar=ln3[3][:, k:k + 1], in1=gms[:, :],
                                               op0=ALU.subtract, op1=ALU.mult)
                a.then_inc(s_lyg, 1)
                dve.wait_ge(s_lyg, 1)
                dve.wait_ge(s_lx1b, 1)
                dve.wait_ge(s_ln3r, c)
                for k in range(NT):
                    a = v.scalar_tensor_tensor(out=last_y[:, k, :], in0=last_y[:, k, :], scalar=ln3[7][:, k:k + 1],
                                               in1=x1[:, j, k, :], op0=ALU.mult, op1=ALU.add)
                    if k % 2 == 1:
                        a.then_inc(s_lyo, 1)

            def row_stats(src, ln, tiles):
                for k in tiles:
                    a = v.bn_stats(ln[0][:, k].rearrange("p a c -> p (a c)"), src(k))
                return a

            def variance(ln, sems, count, stats_count, sign=1.0):
                st, su, dm, mu, va, vb, ve, _ = ln
                s_stats, s_halves, s_parts, s_var = sems
                dve.wait_ge(s_stats, stats_count)
                v.tensor_tensor(su[:, :, :], st[:, :, 0, :], st[:, :, 1, :], ALU.add)
                v.tensor_tensor(dm[:, :], st[:, :, 0, 1], st[:, :, 1, 1], ALU.subtract).then_inc(s_halves, 1)
                dve.wait_ge(s_halves, count)
                v.tensor_scalar(mu[:, :], su[:, :, 1], 0.5 * sign, None, ALU.mult)
                v.tensor_scalar(va[:, :], su[:, :, 2], 1.0 / D, EPS, ALU.mult, ALU.add)
                v.scalar_tensor_tensor(out=vb[:, :], in0=dm[:, :], scalar=0.25, in1=dm[:, :],
                                       op0=ALU.mult, op1=ALU.mult).then_inc(s_parts, 1)
                dve.wait_ge(s_parts, count)
                v.tensor_tensor(ve[:, :], va[:, :], vb[:, :], ALU.add).then_inc(s_var, 1)

            def stats(src, ln, sems, count, sign=1.0):
                row_stats(src, ln, range(NT)).then_inc(sems[0], 1)
                variance(ln, sems, count, count, sign)

            def normalise(dst, src, ln, s_r, s_done, count):
                dve.wait_ge(s_r, count)
                for k in range(NT):
                    a = v.tensor_scalar(dst(k), src(k), ln[3][:, k:k + 1], ln[7][:, k:k + 1], ALU.subtract, ALU.mult)
                a.then_inc(s_done, 1)

            def layernorm1_stats(b, j):
                c = at(b, NJ, j + 1)
                dve.wait_ge(s_x[j], at(b, 16, 16))
                stats(lambda k: xin[:, j, k, :], ln1, (s_ln1s, s_ln1h, s_ln1p, s_ln1v), c, -1.0)
                dve.wait_ge(s_m[j], at(b, 16, 16))
                dve.wait_ge(s_mTp, at(b, NJ, j))
                v.tensor_scalar(mb[:, :, :, :], min_[:, j].rearrange("p k (a s) -> p k a s", a=1).broadcast_to([P, NT, 2, SK]),
                                0, MASKED, ALU.is_equal, ALU.mult).then_inc(s_mb, 1)

            def x_lo(b, j, bank):
                dve.wait_ge(s_qp, at(b, NJ * KD, j * KD))
                for c in range(KD):
                    dve.wait_ge(s_xTh, at(b, NJ * KD, j * KD + c + 1))
                    a = v.tensor_tensor(xTl[:, c, :], ps[:, bank + c, :], xTh[:, c, :].bitcast(F32), ALU.subtract)
                a.then_inc(s_xTl, 1)

            def q_lo(b, j, bank):
                dve.wait_ge(s_qh, at(b, NJ, j + 1))
                for m in range(KD):
                    for par in range(2):
                        r, _ = halves(par)
                        a = v.scalar_tensor_tensor(out=ql[r, 2 * m + par, :], in0=ps[r, bank + m, :], scalar=bqs[r, m:m + 1],
                                                   in1=qh[r, 2 * m + par, :].bitcast(F32), op0=ALU.add, op1=ALU.subtract)
                a.then_inc(s_ql, 1)

            def take_max(b, j, k, banks):
                dve.wait_ge(s_sn, at(b, NJ * NT, j * NT + k + 1))
                bank = banks[k % 2]
                v.tensor_reduce(mx[:, k, :].rearrange("p (a h) -> p a h", a=2),
                                ps[:, bank:bank + 2, :].rearrange("p a (h s) -> p a h s", s=SK),
                                AX.X, ALU.max).then_inc(s_mx, 1)

            def negate_max(b, j):
                dve.wait_ge(s_mx, at(b, NJ * NT, (j + 1) * NT))
                v.tensor_scalar(nm[:, :, 0:H], mx[:, :, :], -1.0, None, ALU.mult).then_inc(s_nmh, 1)
                dve.wait_ge(s_nmh, at(b, NJ, j + 1))
                v.scalar_tensor_tensor(out=nm[:, :, H:2 * H], in0=mx[:, :, :], scalar=-1.0,
                                       in1=nm[:, :, 0:H].bitcast(F32), op0=ALU.mult, op1=ALU.subtract).then_inc(s_nm, 1)

            def invert(b, j):
                dve.wait_ge(s_dn, at(b, NJ, j + 1))
                v.reciprocal(rD[:, :], ps[:, 2, 0:P]).then_inc(s_rd, 1)

            def attn_normalise(b, j):
                dve.wait_ge(s_bc, at(b, NJ, j + 1))
                dve.wait_ge(s_osb, at(b, NJ, j + 1))
                v.tensor_tensor(osb[:, :, :], osb[:, :, :], ps[:, 4:6, :], ALU.mult).then_inc(s_oT, 1)

            def x1_stats(b, j, half):
                c = at(b, NJ, j + 1)
                h = slice(2 * half, 2 * half + 2)
                dve.wait_ge(s_xb, c)
                dve.wait_ge(s_wo, at(b, 2 * NJ, 2 * j + half + 1))
                v.tensor_tensor(x1[:, j, h, :], ps[:, half, :].rearrange("p (k d) -> p k d", d=D), x1[:, j, h, :],
                                ALU.add).then_inc(s_x1, 1)
                dve.wait_ge(s_x1, at(b, 2 * NJ, 2 * j + half + 1))
                row_stats(lambda k: x1[:, j, k, :], ln2, (2 * half, 2 * half + 1)).then_inc(s_ln2s, 1)
                if half:
                    variance(ln2, (s_ln2s, s_ln2h, s_ln2p, s_ln2v), c, 2 * c)

            def layernorm2_apply(b, j, f):
                c = at(b, NJ, j + 1)
                if f:
                    dve.wait_ge(s_xh2f, at(f[0], NJ, f[1] + 1))
                normalise(lambda k: xh2[:, j, k, :], lambda k: x1[:, j, k, :], ln2, s_ln2r, s_ln2, c)

            def mix(b, j, first=0, last=CH, sems=(s_mix1, s_mix2, s_xm), pieces=range(KD)):
                early = last < CH
                dve.wait_ge(s_x2T, at(b, NJ * KD, KD if early else NJ * KD))
                for c in pieces:
                    n = c + 1 if early else at(b, NJ * KD, j * KD + c + 1)
                    t, m = j * CH, slice(first, last)
                    if early:
                        dve.wait_ge(s_xml, at(b, NJ * KD, 0))
                    elif j > 0:
                        dve.wait_ge(s_xml, at(b, NJ * KD, (j - 1) * KD + c + 1))
                        dve.wait_ge(s_xmh, at(b, NJ * KD, (j - 1) * KD + c + 1))
                    v.tensor_scalar(xm[:, c, m], x2T[:, c, t + first:t + last], mks[:, 0, c:c + 1], None, ALU.mult).then_inc(sems[0], 1)
                    dve.wait_ge(sems[0], n)
                    v.scalar_tensor_tensor(out=xm[:, c, m], in0=x2T[:, c, t + 1 + first:t + 1 + last], scalar=mks[:, 1, c:c + 1],
                                           in1=xm[:, c, m], op0=ALU.mult, op1=ALU.add).then_inc(sems[1], 1)
                    dve.wait_ge(sems[1], n)
                    v.scalar_tensor_tensor(out=xm[:, c, m], in0=x2T[:, c, t + 2 + first:t + 2 + last], scalar=mks[:, 2, c:c + 1],
                                           in1=xm[:, c, m], op0=ALU.mult, op1=ALU.add).then_inc(sems[2], 1)

            def early_mix(b):
                mix(b, 0, 0, CH - 1, (s_early1, s_early2, s_early))
                for c in range(KD):
                    dve.wait_ge(s_earlyh, c + 1)
                    v.tensor_tensor(xml[:, c, 0:CH - 1], xm[:, c, 0:CH - 1], xmh[:, c, 0:CH - 1].bitcast(F32), ALU.subtract)

            def mixed_lo(b, j, first=0):
                for c in range(KD):
                    dve.wait_ge(s_xmh, at(b, NJ * KD, j * KD + c + 1))
                    js = slice(j * CH + first, (j + 1) * CH)
                    v.tensor_tensor(xml[:, c, js], xm[:, c, first:], xmh[:, c, js].bitcast(F32), ALU.subtract).then_inc(s_xml, 1)

            def argmax(b, j, L=usual):
                bank = L.bank(j, "gate")
                c = at(b, NJ, j + 1)
                dve.wait_ge(L.s_f, L.filled(b, j, "gate"))
                v.tensor_tensor(gs[:, :, :], ps[:, bank, 0:NT * NPATH].rearrange("p (k n) -> p k n", n=NPATH),
                                bo2s[:, :].rearrange("p (k n) -> p k n", k=1).broadcast_to([P, NT, NPATH]),
                                ALU.add).then_inc(L.s_fv, 1)
                dve.wait_ge(L.s_fv, L.read_by_dve(b, j, 1))
                v.tensor_reduce(gmax[:, :], gs[:, :, :], AX.X, ALU.max).then_inc(s_gmax, 1)
                dve.wait_ge(s_gmax, c)
                iota = cst[:, C_IO:C_IO + NPATH].rearrange("p (k n) -> p k n", k=1).broadcast_to([P, NT, NPATH])

                def per_tile(t):
                    return t[:, :].rearrange("p (k n) -> p k n", n=1).broadcast_to([P, NT, NPATH])

                v.tensor_tensor(cand[:, :, :], gs[:, :, :], per_tile(gmax), ALU.is_ge).then_inc(s_gcand, 1)
                dve.wait_ge(s_gcand, at(b, 2 * NJ, 2 * j + 1))
                v.tensor_tensor(gs[:, :, :], cand[:, :, :], iota, ALU.mult).then_inc(s_gcand, 1)
                dve.wait_ge(s_gcand, at(b, 2 * NJ, 2 * j + 2))
                v.tensor_reduce(gidx[:, :], gs[:, :, :], AX.X, ALU.min).then_inc(s_gidx, 1)
                dve.wait_ge(s_gidx, c)
                v.tensor_tensor(oh[:, :, 0:NPATH], iota, per_tile(gidx), ALU.is_equal).then_inc(s_oh, 1)

            def select(b, j, m, L=usual):
                dve.wait_ge(L.s_fa, L.read_by_act(b, j, min(m + 2, NFA)))
                dve.wait_ge(L.s_f, L.filled(b, j, f"rep{m}"))
                r = rows_of(m)
                v.tensor_tensor(L.selected(m, r), L.h(m, slice(0, r)), ps[0:r, L.bank(j, f"rep{m}"), :],
                                ALU.mult).then_inc(L.s_fv, 1)

            def selected_lo(b, j, m, L=usual):
                dve.wait_ge(L.s_hh, L.count(b, j, NM, m + 1))
                r = rows_of(m)
                v.tensor_tensor(L.lo(m, r), L.selected(m, r), L.hi(m, r).bitcast(F32), ALU.subtract).then_inc(L.s_hl, 1)

            def residual(b, j, half, L=usual):
                c = at(b, NJ, j + 1)
                if half == 0 and L is usual:
                    dve.wait_ge(s_xh2f, c)
                use = ("w2a", "w2b")[half]
                dve.wait_ge(L.s_f, L.filled(b, j, use))
                k = 2 * half
                x = xh2f[:, k:k + 2, :] if L is usual else xh2[:, 1, k:k + 2, :]
                v.tensor_tensor(x, x, ps[:, L.bank(j, use), :].rearrange("p (k d) -> p k d", d=D), ALU.add).then_inc(L.s_fv, 1)

            def residual_stats(b, j, half, L=usual):
                c, k = at(b, NJ, j + 1), 2 * half
                dve.wait_ge(L.s_fv, L.read_by_dve(b, j, NFV - 1 + half))
                row_stats(L.x, ln3, (k, k + 1)).then_inc(s_ln3s, 1)
                if half:
                    variance(ln3, (s_ln3s, s_ln3h, s_ln3p, s_ln3v), c, 2 * c)

            def layernorm3_apply(b, j):
                c = at(b, NJ, j + 1)
                normalise(lambda k: xh2f[:, k, :], lambda k: xh2f[:, k, :], ln3, s_ln3r, s_ln3, c)

            def step(n, front, f, after):
                banks = banks_for_max(n, f)
                if after and not f:
                    layernorm1_stats(*after)
                if front and n:
                    q_lo(*front, 0 if f else 6)
                if f and f[1] == 0:
                    mix(f[0], 1)
                if n and not front:
                    early_mix(n[0])
                if f:
                    argmax(*f)
                if n:
                    invert(*n)
                if after and f:
                    layernorm1_stats(*after)
                if f:
                    select(*f, 0)
                elif front:
                    take_max(*front, 0, banks)
                    take_max(*front, 1, banks)
                if n:
                    attn_normalise(*n)
                if f:
                    select(*f, 1)
                    select(*f, 2)
                    if front:
                        take_max(*front, 0, banks)
                        take_max(*front, 1, banks)
                    select(*f, 3)
                    select(*f, 4)
                    if front:
                        take_max(*front, 2, banks)
                    if n:
                        x1_stats(*n, 0)
                    if front:
                        take_max(*front, 3, banks)
                        negate_max(*front)
                else:
                    if front:
                        take_max(*front, 2, banks)
                        take_max(*front, 3, banks)
                        negate_max(*front)
                    if n:
                        x1_stats(*n, 0)
                if front and not n:
                    q_lo(*front, 6)
                if n:
                    x1_stats(*n, 1)
                    layernorm2_apply(*n, f)
                if f:
                    residual(*f, 0)
                    residual_stats(*f, 0)
                    residual(*f, 1)
                if n and not front:
                    mix(n[0], 0, CH - 1)
                    mixed_lo(n[0], 0, CH - 1)
                if f:
                    residual_stats(*f, 1)
                if n and not front:
                    mix(n[0], 1)
                if after:
                    x_lo(*after, 0 if f else 6)
                if f:
                    layernorm3_apply(*f)
                if n and n[1] == NJ - 1 and front:
                    if not f:
                        dve.wait_ge(s_wf, 16 * WF_LOADS)
                    mix(n[0], 0)
                    mixed_lo(n[0], 0)

            transposed_context_copied()
            layernorm1_stats(0, 0)
            dve.wait_ge(s_ident, 16)
            v.tensor_copy(ident_b[:, :], ident).then_inc(s_id, 1)
            memsets()
            key_weights_repeated()
            constant_rows()
            keys()
            wq_lo()
            x_lo(0, 0, 6)
            values()
            step(None, (0, 0), None, (0, 1))
            step((0, 0), (0, 1), None, (1, 0))
            ffn_weights_lo()
            step((0, 1), (1, 0), None, (1, 1))
            with dve.Fori(1, B - 1) as r:
                step((r, 0), (r, 1), (r - 1, 0), (r + 1, 0))
                step((r, 1), (r + 1, 0), (r - 1, 1), (r + 1, 1))
            step((B - 1, 0), (B - 1, 1), (B - 2, 0), None)
            step((B - 1, 1), None, (B - 2, 1), None)
            f0, f1 = (B - 1, 0), (B - 1, 1)
            v.memset(e[DM:, 4, :], 1.0).then_inc(s_lones, 1)
            dve.wait_ge(s_lones, 1)
            argmax(*f0)
            mixed_lo(*f1)
            select(*f0, 0)
            select(*f0, 1)
            selected_lo(*f0, 0)
            select(*f0, 2)
            selected_lo(*f0, 1)
            select(*f0, 3)
            selected_lo(*f0, 2)
            select(*f0, 4)
            selected_lo(*f0, 3)
            selected_lo(*f0, 4)
            argmax(*f1, last)
            select(*f1, 0, last)
            select(*f1, 1, last)
            selected_lo(*f1, 0, last)
            select(*f1, 2, last)
            selected_lo(*f1, 1, last)
            select(*f1, 3, last)
            selected_lo(*f1, 2, last)
            select(*f1, 4, last)
            selected_lo(*f1, 3, last)
            residual(*f0, 0)
            selected_lo(*f1, 4, last)
            residual_stats(*f0, 0)
            residual(*f0, 1)
            residual_stats(*f0, 1)
            layernorm3_apply(*f0)
            for half in range(2):
                residual(*f1, half, last)
                residual_stats(*f1, half, last)
            last_finish(B - 1, 1)

        @block.gpsimd
        def _(pool):
            g = nc.gpsimd
            g.memset(halfneg[:, :], -0.5).then_inc(s_init, 1)
            g.memset(kml[:, :, :].bitcast(F32), 0.0)
            g.memset(ql[:, :, :].bitcast(F32), 0.0).then_inc(s_init, 1)
            g.memset(spare[:, 0:1], 0.0).then_inc(s_yg, 1)
            g.memset(spare[:, 1:2], 0.0).then_inc(s_yo, 1)
            g.memset(spare[:, 2:3], 0.0).then_inc(s_out[1], 16)
            g.memset(spare[:, 3:4], 0.0).then_inc(s_hl, 1)

            def operands(b):
                pool.wait_ge(s_st, at(b, NJ * NPAIR, 0))

                def keys(src, rows):
                    k = src[rows, bass.ds(b, 1), :]
                    return k.broadcast_to([64, 4, SK])

                def d4(rows):
                    return cst[rows, C_D4:C_D4 + 256].rearrange("p (h s) -> p h s", h=4)

                def to(dst, rows, i):
                    return dst[rows, i, :].rearrange("p (h s) -> p h s", h=4)

                for par in range(2):
                    r, _ = halves(par)
                    g.tensor_tensor(to(kmh, r, par), keys(khi[:, :, :].bitcast(F32), r), d4(r), ALU.mult)
                    g.tensor_tensor(to(kml, r, par), keys(klo, r), d4(r), ALU.mult)
                    for q in (par, par + 2):
                        a = g.tensor_tensor(to(kms, r, q), keys(khi[:, :, :].bitcast(F32), r), d4(r), ALU.mult)
                    a.then_inc(s_km, 1)
                    pool.wait_ge(s_km, at(b, 3, par + 1))

            def value_operand(b):
                pool.wait_ge(s_setup_v, 6)
                pool.wait_ge(s_cst, 16)
                pool.wait_ge(s_dn, at(b, NJ, 0))
                g.tensor_tensor(vd[:, :].rearrange("p (h d) -> p h d", h=2), vall[:, bass.ds(b, 1), :].broadcast_to([P, 2, DK]),
                                cst[:, C_VM:C_VM + 32].rearrange("p (h d) -> p h d", h=2), ALU.mult).then_inc(s_km, 1)

            def rstd(ln, s_v, s_r, c):
                pool.wait_ge(s_v, c)
                g.tensor_tensor(ln[7][:, :], ln[6][:, :], halfneg[:, :], ALU.pow).then_inc(s_r, 1)

            def rstd1(b, j):
                c = at(b, NJ, j + 1)
                rstd(ln1, s_ln1v, s_ln1r, c)
                pool.wait_ge(s_ln1r, c)
                g.tensor_tensor(ln1[5][:, :], ln1[3][:, :], ln1[7][:, :], ALU.mult).then_inc(s_ln1b, 1)

            def add_bo(b, j, f):
                if f:
                    pool.wait_ge(s_x1b, at(f[0], NJ, f[1] + 1))
                pool.wait_ge(s_x[j], at(b, 16, 16))
                g.tensor_tensor(x1[:, j], xin[:, j], bos[:, :].rearrange("p (k d) -> p k d", k=1).broadcast_to([P, NT, D]),
                                ALU.add).then_inc(s_xb, 1)

            def add_beta(b, j):
                pool.wait_ge(s_yo, 1 + at(b, NJ, j))
                g.tensor_tensor(x1b[:, :, :], x1[:, j], bts[:, :].rearrange("p (k d) -> p k d", k=1).broadcast_to([P, NT, D]),
                                ALU.add).then_inc(s_x1b, 1)

            def mixed_lo(b, j):
                for c in range(KD):
                    pool.wait_ge(s_xmh, at(b, NJ * KD, j * KD + c + 1))
                    js = slice(j * CH, (j + 1) * CH)
                    g.tensor_tensor(xml[:, c, js], xm[:, c, :], xmh[:, c, js].bitcast(F32), ALU.subtract).then_inc(s_xml, 1)

            def finish(b, j):
                c = at(b, NJ, j + 1)
                pool.wait_ge(s_ln3, c)
                pool.wait_ge(s_out[1 - j], at(b, 16, 16))
                g.tensor_tensor(y[:, :, :], xh2f[:, :, :], gms[:, :].rearrange("p (k d) -> p k d", k=1).broadcast_to([P, NT, D]),
                                ALU.mult).then_inc(s_yg, 1)
                pool.wait_ge(s_yg, 1 + c)
                pool.wait_ge(s_x1b, c)
                g.tensor_tensor(y[:, :, :], y[:, :, :], x1b[:, :, :], ALU.add).then_inc(s_yo, 1)

            def selected_lo(b, j, m):
                pool.wait_ge(s_hh, usual.count(b, j, NM, m + 1))
                r = rows_of(m)
                g.tensor_tensor(usual.lo(m, r), usual.selected(m, r), usual.hi(m, r).bitcast(F32), ALU.subtract).then_inc(s_hl, 1)

            def step(n, front, f, after):
                if f:
                    add_beta(*f)
                if n:
                    add_bo(*n, f)
                if front and front[1] == 0:
                    operands(front[0])
                if after:
                    rstd1(*after)
                if f and f[1] == 0:
                    mixed_lo(f[0], 1)
                if front and front[1] == 0:
                    value_operand(front[0])
                if f:
                    for m in range(NM):
                        selected_lo(*f, m)
                if n:
                    rstd(ln2, s_ln2v, s_ln2r, at(n[0], NJ, n[1] + 1))
                if f:
                    rstd(ln3, s_ln3v, s_ln3r, at(f[0], NJ, f[1] + 1))
                if f:
                    finish(*f)

            pool.wait_ge(s_init, 2)
            rstd1(0, 0)
            pool.wait_ge(s_setup_v, 5)
            pool.wait_ge(s_kc, 1)
            step(None, (0, 0), None, (0, 1))
            pool.wait_ge(s_wo_in, 32)
            step((0, 0), (0, 1), None, (1, 0))
            pool.wait_ge(s_wf, 16 * WF_LOADS)
            step((0, 1), (1, 0), None, (1, 1))
            with pool.Fori(1, B - 1) as r:
                step((r, 0), (r, 1), (r - 1, 0), (r + 1, 0))
                step((r, 1), (r + 1, 0), (r - 1, 1), (r + 1, 1))
            step((B - 1, 0), (B - 1, 1), (B - 2, 0), None)
            step((B - 1, 1), None, (B - 2, 1), None)
            f0, f1 = (B - 1, 0), (B - 1, 1)
            add_beta(*f0)
            g.tensor_tensor(x1[:, 1], x1[:, 1], bts[:, :].rearrange("p (k d) -> p k d", k=1).broadcast_to([P, NT, D]),
                            ALU.add).then_inc(s_lx1b, 1)
            rstd(ln3, s_ln3v, s_ln3r, at(B - 1, NJ, 1))
            finish(*f0)
            rstd(ln3, s_ln3v, s_ln3r, at(B - 1, NJ, 2))


WK_LOADS = 4
WF_LOADS = KD + 1 + 4 + 3 + 4

_PREFIX = ("L0_xattn_", "L0_ffn_")
_ATTN = ["Wq", "bq", "Wk", "bk", "Wv", "bv", "Wo", "bo"]
_FFN = ["mix_kernel", "W1", "b1", "W2", "b2", "Wo1", "bo1", "Wo2", "bo2", "gamma", "beta"]


def kernel(**inputs):
    from concourse import bacc
    from concourse.bass_utils import run_bass_kernel_spmd

    nc = bacc.Bacc("TRN2", target_bir_lowering=False, num_devices=1)
    names = ["x", "ctx_1024", "mask_Bx1xSxS2_ik1"] + [_PREFIX[0] + n for n in _ATTN] + [_PREFIX[1] + n for n in _FFN]
    arrays = {n: np.ascontiguousarray(inputs[n]) for n in names}
    arrays["constants"] = constants()
    args = [nc.dram_tensor(f"in_{n}", a.shape, mybir.dt.from_np(a.dtype), kind="ExternalInput").ap()
            for n, a in arrays.items()]
    out = nc.dram_tensor("out_0", (B, S, D), F32, kind="ExternalOutput").ap()
    layer_program(nc, *args, out)
    r = run_bass_kernel_spmd(nc, [{f"in_{n}": a for n, a in arrays.items()}], core_ids=[0])
    return r.results[0]["out_0"]
```
